# Optimizing a Trainium2 kernel written in Bass

```python
import numpy as np
import jax
import jax.numpy as jnp

def _softmax(x, axis=-1):
    return jax.nn.softmax(x, axis=axis)

def _gelu(x):
    return jax.nn.gelu(x, approximate=True)

def _silu(x):
    return jax.nn.silu(x)

def _sigmoid(x):
    return jax.nn.sigmoid(x)

def _layernorm(x, axis=-1, eps=1e-05):
    m = jnp.mean(x, axis=axis, keepdims=True)
    v = jnp.var(x, axis=axis, keepdims=True)
    return (x - m) / jnp.sqrt(v + eps)

def _scatter_add(tgt, idx, src, axis=0):
    return tgt.at[idx].add(src)

def _segment_sum(src, seg, n):
    return jax.ops.segment_sum(src, seg, n)
kernel_name = 'mk_rec_standalone_d1_rec_r8_a6b401'

def setup_inputs(seed: int=0):
    np.random.seed(seed)
    _w = jnp.asarray

    def _rec_inputs():
        import jax
        import jax.numpy as jnp
        _rk = jax.random.key(seed)
        r_input_ids = jnp.stack([jax.random.randint(jax.random.fold_in(jax.random.fold_in(_rk, 1), 0), (512,), 87, 199707, jnp.int32), jax.random.randint(jax.random.fold_in(jax.random.fold_in(_rk, 1), 1), (512,), 919, 199903, jnp.int32), jax.random.randint(jax.random.fold_in(jax.random.fold_in(_rk, 1), 2), (512,), 158, 199806, jnp.int32), jax.random.randint(jax.random.fold_in(jax.random.fold_in(_rk, 1), 3), (512,), 1, 199971, jnp.int32), jax.random.randint(jax.random.fold_in(jax.random.fold_in(_rk, 1), 4), (512,), 539, 199213, jnp.int32), jax.random.randint(jax.random.fold_in(jax.random.fold_in(_rk, 1), 5), (512,), 131, 199420, jnp.int32), jax.random.randint(jax.random.fold_in(jax.random.fold_in(_rk, 1), 6), (512,), 81, 199970, jnp.int32), jax.random.randint(jax.random.fold_in(jax.random.fold_in(_rk, 1), 7), (512,), 45, 199853, jnp.int32), jax.random.randint(jax.random.fold_in(jax.random.fold_in(_rk, 1), 8), (512,), 77, 199756, jnp.int32), jax.random.randint(jax.random.fold_in(jax.random.fold_in(_rk, 1), 9), (512,), 126, 24976, jnp.int32), jax.random.randint(jax.random.fold_in(jax.random.fold_in(_rk, 1), 10), (512,), 149, 24964, jnp.int32), jax.random.randint(jax.random.fold_in(jax.random.fold_in(_rk, 1), 11), (512,), 51, 198661, jnp.int32), jax.random.randint(jax.random.fold_in(jax.random.fold_in(_rk, 1), 12), (512,), 430, 198581, jnp.int32), jax.random.randint(jax.random.fold_in(jax.random.fold_in(_rk, 1), 13), (512,), 47, 199740, jnp.int32), jax.random.randint(jax.random.fold_in(jax.random.fold_in(_rk, 1), 14), (512,), 244, 199922, jnp.int32), jax.random.randint(jax.random.fold_in(jax.random.fold_in(_rk, 1), 15), (512,), 633, 199689, jnp.int32), jax.random.randint(jax.random.fold_in(jax.random.fold_in(_rk, 1), 16), (512,), 165, 199301, jnp.int32), jax.random.randint(jax.random.fold_in(jax.random.fold_in(_rk, 1), 17), (512,), 750, 199817, jnp.int32), jax.random.randint(jax.random.fold_in(jax.random.fold_in(_rk, 1), 18), (512,), 76, 199922, jnp.int32), jax.random.randint(jax.random.fold_in(jax.random.fold_in(_rk, 1), 19), (512,), 98, 199990, jnp.int32), jax.random.randint(jax.random.fold_in(jax.random.fold_in(_rk, 1), 20), (512,), 815, 199893, jnp.int32), jax.random.randint(jax.random.fold_in(jax.random.fold_in(_rk, 1), 21), (512,), 764, 199263, jnp.int32), jax.random.randint(jax.random.fold_in(jax.random.fold_in(_rk, 1), 22), (512,), 180, 198859, jnp.int32), jax.random.randint(jax.random.fold_in(jax.random.fold_in(_rk, 1), 23), (512,), 509, 199510, jnp.int32), jax.random.randint(jax.random.fold_in(jax.random.fold_in(_rk, 1), 24), (512,), 799, 199907, jnp.int32), jax.random.randint(jax.random.fold_in(jax.random.fold_in(_rk, 1), 25), (512,), 332, 199638, jnp.int32), jax.random.randint(jax.random.fold_in(jax.random.fold_in(_rk, 1), 26), (512,), 13, 199633, jnp.int32), jax.random.randint(jax.random.fold_in(jax.random.fold_in(_rk, 1), 27), (512,), 1124, 199709, jnp.int32), jax.random.randint(jax.random.fold_in(jax.random.fold_in(_rk, 1), 28), (512,), 352, 24992, jnp.int32), jax.random.randint(jax.random.fold_in(jax.random.fold_in(_rk, 1), 29), (512,), 1229, 199547, jnp.int32), jax.random.randint(jax.random.fold_in(jax.random.fold_in(_rk, 1), 30), (512,), 62, 199806, jnp.int32), jax.random.randint(jax.random.fold_in(jax.random.fold_in(_rk, 1), 31), (512,), 370, 199625, jnp.int32), jax.random.randint(jax.random.fold_in(jax.random.fold_in(_rk, 1), 32), (512,), 413, 199070, jnp.int32), jax.random.randint(jax.random.fold_in(jax.random.fold_in(_rk, 1), 33), (512,), 451, 199750, jnp.int32), jax.random.randint(jax.random.fold_in(jax.random.fold_in(_rk, 1), 34), (512,), 145, 199693, jnp.int32), jax.random.randint(jax.random.fold_in(jax.random.fold_in(_rk, 1), 35), (512,), 60, 199284, jnp.int32), jax.random.randint(jax.random.fold_in(jax.random.fold_in(_rk, 1), 36), (512,), 177, 199809, jnp.int32), jax.random.randint(jax.random.fold_in(jax.random.fold_in(_rk, 1), 37), (512,), 944, 199566, jnp.int32), jax.random.randint(jax.random.fold_in(jax.random.fold_in(_rk, 1), 38), (512,), 233, 24898, jnp.int32), jax.random.randint(jax.random.fold_in(jax.random.fold_in(_rk, 1), 39), (512,), 361, 199887, jnp.int32), jax.random.randint(jax.random.fold_in(jax.random.fold_in(_rk, 1), 40), (512,), 355, 199964, jnp.int32), jax.random.randint(jax.random.fold_in(jax.random.fold_in(_rk, 1), 41), (512,), 301, 199862, jnp.int32), jax.random.randint(jax.random.fold_in(jax.random.fold_in(_rk, 1), 42), (512,), 33, 24998, jnp.int32), jax.random.randint(jax.random.fold_in(jax.random.fold_in(_rk, 1), 43), (512,), 42, 199836, jnp.int32), jax.random.randint(jax.random.fold_in(jax.random.fold_in(_rk, 1), 44), (512,), 151, 24933, jnp.int32), jax.random.randint(jax.random.fold_in(jax.random.fold_in(_rk, 1), 45), (512,), 116, 199163, jnp.int32), jax.random.randint(jax.random.fold_in(jax.random.fold_in(_rk, 1), 46), (512,), 448, 199962, jnp.int32), jax.random.randint(jax.random.fold_in(jax.random.fold_in(_rk, 1), 47), (512,), 72, 199690, jnp.int32), jax.random.randint(jax.random.fold_in(jax.random.fold_in(_rk, 1), 48), (512,), 475, 199514, jnp.int32), jax.random.randint(jax.random.fold_in(jax.random.fold_in(_rk, 1), 49), (512,), 72, 199500, jnp.int32), jax.random.randint(jax.random.fold_in(jax.random.fold_in(_rk, 1), 50), (512,), 8, 199990, jnp.int32), jax.random.randint(jax.random.fold_in(jax.random.fold_in(_rk, 1), 51), (512,), 483, 199844, jnp.int32), jax.random.randint(jax.random.fold_in(jax.random.fold_in(_rk, 1), 52), (512,), 16, 24997, jnp.int32), jax.random.randint(jax.random.fold_in(jax.random.fold_in(_rk, 1), 53), (512,), 695, 24942, jnp.int32), jax.random.randint(jax.random.fold_in(jax.random.fold_in(_rk, 1), 54), (512,), 441, 199915, jnp.int32), jax.random.randint(jax.random.fold_in(jax.random.fold_in(_rk, 1), 55), (512,), 1838, 199987, jnp.int32), jax.random.randint(jax.random.fold_in(jax.random.fold_in(_rk, 1), 56), (512,), 787, 199580, jnp.int32), jax.random.randint(jax.random.fold_in(jax.random.fold_in(_rk, 1), 57), (512,), 149, 199670, jnp.int32), jax.random.randint(jax.random.fold_in(jax.random.fold_in(_rk, 1), 58), (512,), 336, 198646, jnp.int32), jax.random.randint(jax.random.fold_in(jax.random.fold_in(_rk, 1), 59), (512,), 94, 199887, jnp.int32), jax.random.randint(jax.random.fold_in(jax.random.fold_in(_rk, 1), 60), (512,), 30, 199209, jnp.int32), jax.random.randint(jax.random.fold_in(jax.random.fold_in(_rk, 1), 61), (512,), 69, 199815, jnp.int32), jax.random.randint(jax.random.fold_in(jax.random.fold_in(_rk, 1), 62), (512,), 681, 199279, jnp.int32), jax.random.randint(jax.random.fold_in(jax.random.fold_in(_rk, 1), 63), (512,), 320, 199181, jnp.int32)], axis=1)
        return r_input_ids
    r_input_ids = _rec_inputs()

    def _L0_rec_setup():
        import jax, jax.numpy as jnp
        import numpy as np
        NUM_ITEMS = 25000
        B = 512
        S = 64
        D = 64
        H = 1
        NBLOCKS = 2
        EPS = 0.001
        NEG = -2.0 ** 32 + 1.0

        def _layernorm(x, g, b):
            mu = jnp.mean(x, -1, keepdims=True)
            var = jnp.var(x, -1, keepdims=True)
            return (x - mu) * jax.lax.rsqrt(var + EPS) * g + b

        def _mha(queries, keys, Wq, bq, Wk, bk, Wv, bv):
            Bq, Sq, Dm = queries.shape
            dh = Dm // H

            def split(x):
                return x.reshape(Bq, Sq, H, dh).transpose(0, 2, 1, 3)
            Q = split(queries @ Wq + bq)
            K = split(keys @ Wk + bk)
            V = split(keys @ Wv + bv)
            scores = jnp.einsum('bhqd,bhkd->bhqk', Q, K) / jnp.sqrt(jnp.float32(dh))
            key_mask = jnp.sign(jnp.abs(jnp.sum(keys, -1)))
            scores = jnp.where(key_mask[:, None, None, :] == 0, NEG, scores)
            causal = jnp.tril(jnp.ones((Sq, Sq), jnp.float32))
            scores = jnp.where(causal[None, None] == 0, NEG, scores)
            attn = jax.nn.softmax(scores, axis=-1)
            query_mask = jnp.sign(jnp.abs(jnp.sum(queries, -1)))
            attn = attn * query_mask[:, None, :, None]
            out = jnp.einsum('bhqk,bhkd->bhqd', attn, V)
            return out.transpose(0, 2, 1, 3).reshape(Bq, Sq, Dm)
        key = jax.random.key(seed)
        ks = jax.random.split(key, 12)

        def nrm(k, shape, s=0.02):
            return jax.random.normal(k, shape, dtype=jnp.float32) * s
        return {'input_ids': jax.random.randint(ks[0], (B, S), 0, NUM_ITEMS + 1), 'item_emb': nrm(ks[1], (NUM_ITEMS + 1, D)), 'pos_emb': nrm(ks[2], (S, D)), 'ln1_g': jnp.ones((NBLOCKS, D), jnp.float32), 'ln1_b': jnp.zeros((NBLOCKS, D), jnp.float32), 'Wq': nrm(ks[3], (NBLOCKS, D, D)), 'bq': jnp.zeros((NBLOCKS, D), jnp.float32), 'Wk': nrm(ks[4], (NBLOCKS, D, D)), 'bk': jnp.zeros((NBLOCKS, D), jnp.float32), 'Wv': nrm(ks[5], (NBLOCKS, D, D)), 'bv': jnp.zeros((NBLOCKS, D), jnp.float32), 'ln2_g': jnp.ones((NBLOCKS, D), jnp.float32), 'ln2_b': jnp.zeros((NBLOCKS, D), jnp.float32), 'W1': nrm(ks[6], (NBLOCKS, D, D)), 'b1': jnp.zeros((NBLOCKS, D), jnp.float32), 'W2': nrm(ks[7], (NBLOCKS, D, D)), 'b2': jnp.zeros((NBLOCKS, D), jnp.float32), 'lnf_g': jnp.ones((D,), jnp.float32), 'lnf_b': jnp.zeros((D,), jnp.float32), 'out_item_emb': nrm(ks[8], (NUM_ITEMS, D))}
    _L0_rec_all = _L0_rec_setup()
    _L0_rec_in = {k: v for k, v in _L0_rec_all.items() if k in ('item_emb', 'pos_emb', 'ln1_g', 'ln1_b', 'Wq', 'bq', 'Wk', 'bk', 'Wv', 'bv', 'ln2_g', 'ln2_b', 'W1', 'b1', 'W2', 'b2', 'lnf_g', 'lnf_b', 'out_item_emb')}
    del _L0_rec_all
    return {'r_input_ids': r_input_ids, 'L0_rec_item_emb': _L0_rec_in['item_emb'], 'L0_rec_pos_emb': _L0_rec_in['pos_emb'], 'L0_rec_ln1_g': _L0_rec_in['ln1_g'], 'L0_rec_ln1_b': _L0_rec_in['ln1_b'], 'L0_rec_Wq': _L0_rec_in['Wq'], 'L0_rec_bq': _L0_rec_in['bq'], 'L0_rec_Wk': _L0_rec_in['Wk'], 'L0_rec_bk': _L0_rec_in['bk'], 'L0_rec_Wv': _L0_rec_in['Wv'], 'L0_rec_bv': _L0_rec_in['bv'], 'L0_rec_ln2_g': _L0_rec_in['ln2_g'], 'L0_rec_ln2_b': _L0_rec_in['ln2_b'], 'L0_rec_W1': _L0_rec_in['W1'], 'L0_rec_b1': _L0_rec_in['b1'], 'L0_rec_W2': _L0_rec_in['W2'], 'L0_rec_b2': _L0_rec_in['b2'], 'L0_rec_lnf_g': _L0_rec_in['lnf_g'], 'L0_rec_lnf_b': _L0_rec_in['lnf_b'], 'L0_rec_out_item_emb': _L0_rec_in['out_item_emb']}

def reference(r_input_ids, L0_rec_item_emb, L0_rec_pos_emb, L0_rec_ln1_g, L0_rec_ln1_b, L0_rec_Wq, L0_rec_bq, L0_rec_Wk, L0_rec_bk, L0_rec_Wv, L0_rec_bv, L0_rec_ln2_g, L0_rec_ln2_b, L0_rec_W1, L0_rec_b1, L0_rec_W2, L0_rec_b2, L0_rec_lnf_g, L0_rec_lnf_b, L0_rec_out_item_emb):
    import jax
    import jax.numpy as jnp

    def _L0_rec_ref(input_ids, item_emb, pos_emb, ln1_g, ln1_b, Wq, bq, Wk, bk, Wv, bv, ln2_g, ln2_b, W1, b1, W2, b2, lnf_g, lnf_b, out_item_emb):
        import jax, jax.numpy as jnp
        import numpy as np
        NUM_ITEMS = 25000
        B = 512
        S = 64
        D = 64
        H = 1
        NBLOCKS = 2
        EPS = 0.001
        NEG = -2.0 ** 32 + 1.0

        def _layernorm(x, g, b):
            mu = jnp.mean(x, -1, keepdims=True)
            var = jnp.var(x, -1, keepdims=True)
            return (x - mu) * jax.lax.rsqrt(var + EPS) * g + b

        def _mha(queries, keys, Wq, bq, Wk, bk, Wv, bv):
            Bq, Sq, Dm = queries.shape
            dh = Dm // H

            def split(x):
                return x.reshape(Bq, Sq, H, dh).transpose(0, 2, 1, 3)
            Q = split(queries @ Wq + bq)
            K = split(keys @ Wk + bk)
            V = split(keys @ Wv + bv)
            scores = jnp.einsum('bhqd,bhkd->bhqk', Q, K) / jnp.sqrt(jnp.float32(dh))
            key_mask = jnp.sign(jnp.abs(jnp.sum(keys, -1)))
            scores = jnp.where(key_mask[:, None, None, :] == 0, NEG, scores)
            causal = jnp.tril(jnp.ones((Sq, Sq), jnp.float32))
            scores = jnp.where(causal[None, None] == 0, NEG, scores)
            attn = jax.nn.softmax(scores, axis=-1)
            query_mask = jnp.sign(jnp.abs(jnp.sum(queries, -1)))
            attn = attn * query_mask[:, None, :, None]
            out = jnp.einsum('bhqk,bhkd->bhqd', attn, V)
            return out.transpose(0, 2, 1, 3).reshape(Bq, Sq, Dm)
        mask = (input_ids != NUM_ITEMS).astype(jnp.float32)[..., None]
        seq = item_emb[input_ids] + pos_emb[None]
        seq = seq * mask
        for i in range(NBLOCKS):
            x = _layernorm(seq, ln1_g[i], ln1_b[i])
            q = x
            x = _mha(q, seq, Wq[i], bq[i], Wk[i], bk[i], Wv[i], bv[i])
            x = x + q
            x = _layernorm(x, ln2_g[i], ln2_b[i])
            res = x
            x = jax.nn.relu(x @ W1[i] + b1[i]) @ W2[i] + b2[i]
            x = x + res
            seq = x * mask
        seq_emb = _layernorm(seq, lnf_g, lnf_b)[:, -1, :]
        return seq_emb @ out_item_emb.T
    y = _L0_rec_ref(r_input_ids, L0_rec_item_emb, L0_rec_pos_emb, L0_rec_ln1_g, L0_rec_ln1_b, L0_rec_Wq, L0_rec_bq, L0_rec_Wk, L0_rec_bk, L0_rec_Wv, L0_rec_bv, L0_rec_ln2_g, L0_rec_ln2_b, L0_rec_W1, L0_rec_b1, L0_rec_W2, L0_rec_b2, L0_rec_lnf_g, L0_rec_lnf_b, L0_rec_out_item_emb)
    return y

_drawn_inputs = setup_inputs


def setup_inputs(seed=0):
    import zlib

    import numpy as np

    out = dict(_drawn_inputs(seed))
    spreads = {'L0_rec_ln1_g': (1.0, 0.2),
     'L0_rec_ln1_b': (0.0, 0.1),
     'L0_rec_bq': (0.0, 2.0),
     'L0_rec_bk': (0.0, 2.0),
     'L0_rec_bv': (0.0, 0.1),
     'L0_rec_ln2_g': (1.0, 0.2),
     'L0_rec_ln2_b': (0.0, 0.1),
     'L0_rec_b1': (0.0, 0.609),
     'L0_rec_b2': (0.0, 0.1),
     'L0_rec_lnf_g': (1.0, 0.2),
     'L0_rec_lnf_b': (0.0, 0.1)}
    factors = {'L0_rec_Wq': 8.0, 'L0_rec_Wk': 8.0, 'L0_rec_W1': 2.687}
    for name, (base, spread) in spreads.items():
        noise = np.random.default_rng([zlib.crc32(name.encode()), seed]).standard_normal(out[name].shape)
        drawn = base * np.exp(spread * noise) if base else spread * noise
        out[name] = jnp.asarray(drawn.astype(out[name].dtype))
    for name, factor in factors.items():
        out[name] = (out[name] * factor).astype(out[name].dtype)
    return out
```

```python
from contextlib import ExitStack

import concourse.bass as bass
from concourse import mybir

F32 = mybir.dt.float32
BF16 = mybir.dt.bfloat16
I32 = mybir.dt.int32
ALU = mybir.AluOpType
ACT = mybir.ActivationFunctionType
AX = mybir.AxisListType

P = 128
D = 64
EPS = 0.001
NEG = -2.0 ** 32
KEY_OFF = -2.0 ** 100
U = 4
J = 4
W = J * P
T = 2 * J
ROWS = 32

(LN1G0, LN1B0, BQ0, BK0, LN2G0, LN2B0, B10, B20,
 LN1G1, LN1B1, BQ1, BV1, LN2G1, LN2B1, B11, B21, LNFG, LNFB, BK1, NVEC) = range(20)
WQ0, WK0, WV0, W10, W20, WQ1, WKT1, WV1, W11, W21, NW = range(11)


def build(nc, ids_tok, ids_last, item_emb, vecs, weights, pos, bv_row, g_row, b_row, items_t,
          ident_c, center_c, mean_c, causal_c, diag2_c, sel1_c, sel2_c, out):
    n_tiles = ids_tok.shape[1]
    STEPS = n_tiles // (U * T)
    NITEMS = items_t.shape[1]
    B = out.shape[0]
    NROW = item_emb.shape[0]
    QL = B // 2
    LC = U * J * 2

    with ExitStack() as ctx:
        def sb(name, shape, dt=F32):
            return ctx.enter_context(nc.sbuf_tensor(name, shape, dt))

        def sem(name):
            return ctx.enter_context(nc.semaphore(name))

        banks = [ctx.enter_context(nc.psum_tensor(f"bank{i}", [P, 512], F32)) for i in range(8)]
        lo, hi = banks[:4], banks[4:]

        ident = sb("ident", [P, P])
        center = sb("center", [P, P])
        mean_m = sb("mean_m", [P, P])
        causal = sb("causal", [P, D])
        diag2 = sb("diag2", [P, W])
        sel1f = sb("sel1f", [U * T, U * J * P])
        sel1 = sb("sel1", [U * T, U * J * P], BF16)
        sel2f = sb("sel2f", [U * T, J * P])
        sel2 = sb("sel2", [U * T, J * P], BF16)
        vec = sb("vec", [P, NVEC])
        vec8 = sb("vec8", [P, 2])
        wbd = sb("wbd", [P, NW, P])
        wmean = sb("wmean", [P, 4])
        pos2 = sb("pos2", [P, D])
        bvr = sb("bvr", [P, D])
        gr = sb("gr", [P, D])
        br = sb("br", [P, D])
        bsum = sb("bsum", [P, 1])
        bkrep = sb("bkrep", [P, W])
        half_neg = sb("half_neg", [P, LC])
        ids_i = sb("ids_i", [P, n_tiles], I32)
        ids_f = sb("ids_f", [P, n_tiles])
        ids_n = sb("ids_n", [P, n_tiles])
        idx = sb("idx", [P, n_tiles], I32)
        idx_now = sb("idx_now", [P, U * T], I32)
        mask = sb("mask", [P, n_tiles])
        idl_i = sb("idl_i", [P, QL], I32)
        mlast = sb("mlast", [P, QL])

        emb = sb("emb", [P, U, W])
        seq = sb("seq", [P, U, W])
        seqT = sb("seqT", [P, U, W])
        KT = sb("KT", [P, U, W])
        V = sb("V", [P, U, W])
        xn = sb("xn", [P, U, W])
        xT = sb("xT", [P, U, W])
        QT = sb("QT", [P, U, W])
        att = sb("att", [P, U, W])
        PT = sb("PT", [P, U, W])
        x2T = sb("x2T", [P, U, W])
        HT = sb("HT", [P, U, W])
        seq2T = sb("seq2T", [P, U, W])
        seq2 = sb("seq2", [P, U, W])
        stat = sb("stat", [P, U, T, 6])
        st = sb("st", [P, U, 10, T])
        koff = sb("koff", [P, U * T])
        koffT = sb("koffT", [U * T, P], BF16)
        koff2 = sb("koff2", [P, U * T])
        koffT2 = sb("koffT2", [U * T, P], BF16)

        xl = sb("xl", [P, 6, LC])
        QB = sb("QB", [P, U, ROWS])
        AB = sb("AB", [P, U, ROWS])
        s2 = sb("s2", [P, W])
        s2v = sb("s2v", [P, 4])
        PT2 = sb("PT2", [P, W])
        o2 = sb("o2", [P, P])
        XL = sb("XL", [P, QL])
        OT = sb("OT", [P, QL])

        s_const = sem("s_const")
        s_zero = sem("s_zero")
        s_prep = sem("s_prep")
        s_idx = sem("s_idx")
        s_now = sem("s_now")
        s_gath = [sem(f"s_gath{u}") for u in range(U)]
        s_room = sem("s_room")
        s_raw = sem("s_raw")
        s_seq = sem("s_seq")
        s_stat = sem("s_stat")
        s_var = sem("s_var")
        s_rstd = sem("s_rstd")
        s_koff = sem("s_koff")
        s_xn = sem("s_xn")
        s_xg = sem("s_xg")
        s_qsum = sem("s_qsum")
        s_qm = sem("s_qm")
        p_seqT = sem("p_seqT")
        s_seqT = sem("s_seqT")
        p_K = sem("p_K")
        s_K = sem("s_K")
        p_V = sem("p_V")
        s_V = sem("s_V")
        p_koff = sem("p_koff")
        s_koffT = sem("s_koffT")
        p_xT = sem("p_xT")
        s_xT = sem("s_xT")
        p_Q = sem("p_Q")
        s_Q = sem("s_Q")
        p_S = sem("p_S")
        s_S = sem("s_S")
        s_max = sem("s_max")
        s_sub = sem("s_sub")
        s_exp = sem("s_exp")
        s_sum = sem("s_sum")
        s_inv = sem("s_inv")
        s_P = sem("s_P")
        p_PT = sem("p_PT")
        s_PT = sem("s_PT")
        p_z = sem("p_z")
        s_sq = sem("s_sq")
        s_ss = sem("s_ss")
        s_var2 = sem("s_var2")
        s_rstd2 = sem("s_rstd2")
        s_zn = sem("s_zn")
        p_x2T = sem("p_x2T")
        s_x2T = sem("s_x2T")
        p_H = sem("p_H")
        s_H = sem("s_H")
        p_Y = sem("p_Y")
        s_seq2T = sem("s_seq2T")
        p_seq2 = sem("p_seq2")
        s_seq2 = sem("s_seq2")
        s_koff2 = sem("s_koff2")
        c_last = sem("c_last")
        c_pc = sem("c_pc")
        c_cen = sem("c_cen")
        c_sq = sem("c_sq")
        c_pv = sem("c_pv")
        c_var = sem("c_var")
        c_rstd = sem("c_rstd")
        c_xn = sem("c_xn")
        c_x = sem("c_x")
        c_pq = sem("c_pq")
        c_QB = sem("c_QB")
        c_pa = sem("c_pa")
        c_AB = sem("c_AB")
        c_pk = sem("c_pk")
        c_kT = sem("c_kT")
        c_pS = sem("c_pS")
        c_S = sem("c_S")
        c_dve = sem("c_dve")
        c_exp = sem("c_exp")
        c_P = sem("c_P")
        c_pPT = sem("c_pPT")
        c_PT = sem("c_PT")
        c_pO = sem("c_pO")
        c_O = sem("c_O")
        c_pOT = sem("c_pOT")
        c_OT = sem("c_OT")

        za = seq[:, 0, 0:QL]
        zc = seq[:, 1, 0:QL]
        zs = seq[:, 2, 0:QL]
        zv = seq[:, 3, 0:QL]
        zr = xn[:, 0, 0:QL]
        zn = xn[:, 1, 0:QL]
        zx = xn[:, 2, 0:QL]
        zh = xn[:, 3, 0:QL]
        zy = att[:, 0, 0:QL]
        zt = x2T[:, 0, 0:QL]
        qml = att[:, 1, 0:QL]
        FT = att[:, 2, :]
        FR = att[:, 3, :]
        FM = PT[:, 0, :]
        f_hi = sb("f_hi", [P, B], BF16)
        f_mid = sb("f_mid", [P, B], BF16)
        f_hl = sb("f_hl", [P, B], BF16)
        NB = 500
        NC = 1000
        CH = NITEMS // NC
        NT = B // P
        it32 = [emb[:, 0:2, :].rearrange("p a b -> p (a b)")[:, 0:NC],
                emb[:, 2:4, :].rearrange("p a b -> p (a b)")[:, 0:NC]]
        irem = [seqT[:, 0:2, :].rearrange("p a b -> p (a b)")[:, 0:NC],
                seqT[:, 2:4, :].rearrange("p a b -> p (a b)")[:, 0:NC]]
        ihi = [sb(f"ihi{i}", [P, NC], BF16) for i in range(2)]
        imid = [sb(f"imid{i}", [P, NC], BF16) for i in range(2)]
        ix = [sb(f"ix{i}", [P, NC], BF16) for i in range(2)]
        iy = [sb(f"iy{i}", [P, NC], BF16) for i in range(2)]
        ost = [(KT, V, QT, HT)[i][:, 2 * k:2 * k + 2, :].rearrange("p a b -> p (a b)")[:, 0:NC]
               for k in range(2) for i in range(4)]
        e_go = sem("e_go")
        e_pe = sem("e_pe")
        e_dve = sem("e_dve")
        e_act = sem("e_act")
        e_var = sem("e_var")
        f_split = sem("f_split")
        i_load = [sem(f"i_load{i}") for i in range(2)]
        i_hi = sem("i_hi")
        i_rem = sem("i_rem")
        i_mid = sem("i_mid")
        i_cast = sem("i_cast")
        i_xy = sem("i_xy")
        i_mm = sem("i_mm")
        o_even = sem("o_even")
        o_odd = sem("o_odd")
        o_st = [sem(f"o_st{i}") for i in range(2)]

        block = ctx.enter_context(nc.Block())

        def v1(c, h=None):
            return vec[:, c:c + 1] if h is None else vec[D * h:D * h + D, c:c + 1]

        def tiles(buf, u):
            return buf[:, u, :].rearrange("p (t f) -> p t f", f=D)

        def spread(small):
            return small.unsqueeze(2).broadcast_to([P, T, D])

        n_const = [0]
        n_prep = [0]

        @block.sync
        def _(sp):
            def load(dst, src):
                sp.dma_start(dst, src).then_inc(s_const, 16)
                n_const[0] += 16
            load(ids_i[:, :], ids_tok)
            for h in range(2):
                load(idl_i[D * h:D * h + D, :], ids_last[h:h + 1, :].broadcast_to([D, QL]))
            load(ident[:, :], ident_c)
            load(center[:, :], center_c)
            load(mean_m[:, :], mean_c)
            load(causal[:, :], causal_c)
            load(diag2[:, :], diag2_c)
            load(sel1f[:, :], sel1_c)
            load(sel2f[:, :], sel2_c)
            for h in range(2):
                load(vec[D * h:D * h + D, :], vecs)
                load(pos2[D * h:D * h + D, :], pos)
            load(bvr[:, :], bv_row.broadcast_to([P, D]))
            load(gr[:, :], g_row.broadcast_to([P, D]))
            load(br[:, :], b_row.broadcast_to([P, D]))
            sp.wait_ge(s_zero, 1)
            for h in range(2):
                load(wbd[D * h:D * h + D, :, D * h:D * h + D], weights)

            sp.wait_ge(e_go, 1)
            for c in range(2):
                for h in range(2):
                    sp.dma_start(it32[c][D * h:D * h + D, :],
                                 items_t[:, c * NC:c * NC + NC]).then_inc(i_load[c], 16)

            def step(c2, k, more):
                c = c2 * 2 + k
                if more:
                    sp.wait_ge(i_rem, c + 1)
                    sp.wait_ge(i_hi, c + 1)
                    for h in range(2):
                        sp.dma_start(it32[k][D * h:D * h + D, :],
                                     items_t[:, bass.ds((c + 2) * NC, NC)]).then_inc(i_load[k], 16)
                for t in range(NT):
                    sp.wait_ge(o_even, (c * NT + t) + 1)
                    sp.wait_ge(o_odd, (c * NT + t) + 1)
                    sp.dma_start(out[P * t:P * t + P, bass.ds(c * NC, NC)],
                                 ost[k * NT + t]).then_inc(o_st[k], 16)

            with sp.Fori(0, (CH - 3) // 2) as c2:
                step(c2, 0, True)
                step(c2, 1, True)
            last = (CH - 3) // 2
            step(last, 0, True)
            step(last, 1, False)
            step(last + 1, 0, False)
            for k in range(2):
                sp.wait_ge(o_st[k], 16 * NT * ((CH + 1 - k) // 2))

        @block.gpsimd
        def _(pool):
            pool.memset(wbd[:, :, :], 0.0).then_inc(s_zero, 1)
            pool.memset(QB[:, :, :], 0.0).then_inc(s_zero, 1)
            pool.memset(half_neg[:, :], -0.5).then_inc(s_zero, 1)

            def gather(it):
                pool.tensor_copy(idx_now[:, :], idx[:, bass.ds(it * (U * T), U * T)]).then_inc(s_now, 1)
                for u in range(U):
                    n = it * U + u
                    if u == 0:
                        pool.wait_ge(s_now, it + 1)
                    pool.wait_ge(s_raw, n + 1)
                    pool.sem_inc(s_room, 1)
                    for t in range(T):
                        pool.indirect_dma_start(
                            out=emb[:, u, D * t:D * t + D], out_offset=None, in_=item_emb,
                            in_offset=bass.IndirectOffsetOnAxis(ap=idx_now[:, u * T + t:u * T + t + 1], axis=0),
                        ).then_inc(s_gath[u], 16)

            def rstd1(it):
                for u in range(U):
                    n = it * U + u
                    pool.wait_ge(s_var, n + 1)
                    pool.tensor_tensor(st[:, u, 1, :], st[:, u, 0, :], half_neg[:, 0:T], ALU.pow).then_inc(s_rstd, 1)

            def rstd2(it):
                for u in range(U):
                    n = it * U + u
                    pool.wait_ge(s_var2, n + 1)
                    pool.tensor_tensor(st[:, u, 8, :], st[:, u, 7, :], half_neg[:, 0:T], ALU.pow).then_inc(s_rstd2, 1)
                pool.wait_ge(c_var, it + 1)
                pool.tensor_tensor(xl[:, 4, :], xl[:, 3, :], half_neg[:, 0:LC], ALU.pow).then_inc(c_rstd, 1)

            pool.wait_ge(s_idx, 1)
            pool.wait_ge(s_zero, 3)
            gather(0)
            with pool.Fori(0, STEPS - 1) as it:
                rstd1(it)
                for u in range(U):
                    pool.wait_ge(s_gath[u], (it + 1) * (16 * T))
                gather(it + 1)
                rstd2(it)
            rstd1(STEPS - 1)
            rstd2(STEPS - 1)

        @block.vector
        def _(dve):
            step_no = n_prep

            def prep(ins):
                step_no[0] += 1
                ins.then_inc(s_prep, 1)
                dve.wait_ge(s_prep, step_no[0])

            dve.sem_inc(s_raw, U)

            dve.wait_ge(s_const, n_const[0])
            prep(dve.tensor_copy(ids_f[:, :], ids_i[:, :]))
            prep(dve.tensor_scalar(mask[:, :], ids_f[:, :], float(NROW - 1), None, ALU.not_equal))
            prep(dve.tensor_scalar(ids_n[:, :], ids_f[:, :], 0.0, float(NROW), ALU.is_lt, ALU.mult))
            prep(dve.tensor_tensor(ids_f[:, :], ids_f[:, :], ids_n[:, :], ALU.add))
            prep(dve.tensor_scalar(ids_f[:, :], ids_f[:, :], 0.0, float(NROW - 1), ALU.max, ALU.min))
            dve.tensor_copy(idx[:, :], ids_f[:, :]).then_inc(s_idx, 1)
            prep(dve.tensor_scalar(mlast[:, :], idl_i[:, :], float(NROW - 1), None, ALU.not_equal))
            prep(dve.tensor_copy(sel1[:, :], sel1f[:, :]))
            prep(dve.tensor_copy(sel2[:, :], sel2f[:, :]))
            prep(dve.tensor_scalar(vec8[:, 0:1], v1(BQ0), 0.125, None, ALU.mult))
            prep(dve.tensor_scalar(vec8[:, 1:2], v1(BQ1), 0.125, None, ALU.mult))
            for h in range(2):
                a, b = D * h, D * h + D
                blk = wbd[a:b, WV0, a:b]
                prep(dve.tensor_reduce(wmean[a:b, 0:1], blk, AX.X, ALU.add))
                prep(dve.tensor_scalar(wmean[a:b, 1:2], wmean[a:b, 0:1], 1.0 / D, None, ALU.mult))
                prep(dve.tensor_scalar(blk, blk, wmean[a:b, 1:2], None, ALU.subtract))
            prep(dve.tensor_reduce(wmean[:, 2:3], bvr[:, :], AX.X, ALU.add))
            prep(dve.tensor_scalar(wmean[:, 3:4], wmean[:, 2:3], 1.0 / D, None, ALU.mult))
            prep(dve.tensor_scalar(bvr[:, :], bvr[:, :], wmean[:, 3:4], None, ALU.subtract))
            prep(dve.tensor_reduce(bsum[:, :], br[:, :], AX.X, ALU.add))
            prep(dve.memset(bkrep[:, :], 0.0))
            prep(dve.tensor_scalar(bkrep[:, :], bkrep[:, :], v1(BK1), None, ALU.add))

            causal_b = causal[:, :].unsqueeze(1).broadcast_to([P, T, D])
            bv_b = bvr[:, :].unsqueeze(1).broadcast_to([P, T, D])
            g_b = gr[:, :].unsqueeze(1).broadcast_to([P, T, D])
            pos_b = pos2[:, :].unsqueeze(1).broadcast_to([P, T, D])

            def loop(it):
                count = [0]

                def chain(ins):
                    count[0] += 1
                    ins.then_inc(s_stat, 1)
                    dve.wait_ge(s_stat, it * CHAIN + count[0])

                for u in range(U):
                    n = it * U + u
                    m = mask[:, bass.ds(n * T, T)]
                    dve.wait_ge(s_gath[u], (it + 1) * (16 * T))
                    dve.tensor_tensor(tiles(seq, u), tiles(emb, u), pos_b, ALU.add).then_inc(s_raw, 1)
                    dve.wait_ge(s_raw, n + 1 + U)
                    dve.tensor_tensor(tiles(seq, u), tiles(seq, u), spread(m), ALU.mult).then_inc(s_seq, 1)
                for u in range(U):
                    n = it * U + u
                    dve.wait_ge(s_seq, n + 1)
                    for t in range(T):
                        last = dve.bn_stats(stat[:, u, t, :], seq[:, u, D * t:D * t + D])
                    chain(last)
                    me, Me = stat[:, u, :, 1], stat[:, u, :, 2]
                    mo, Mo = stat[:, u, :, 4], stat[:, u, :, 5]
                    dve.tensor_tensor(st[:, u, 2, :], me, mo, ALU.add).then_inc(s_koff, 1)
                    dve.tensor_tensor(st[:, u, 3, :], me, mo, ALU.subtract)
                    chain(dve.tensor_tensor(st[:, u, 4, :], Me, Mo, ALU.add))
                    dve.tensor_scalar(koff[:, u * T:u * T + T], st[:, u, 2, :], 0.0, KEY_OFF,
                                      ALU.is_equal, ALU.mult).then_inc(s_koff, 1)
                    dve.tensor_scalar(st[:, u, 5, :], st[:, u, 2, :], 0.5, None, ALU.mult)
                    chain(dve.tensor_tensor(st[:, u, 3, :], st[:, u, 3, :], st[:, u, 3, :], ALU.mult))
                    chain(dve.scalar_tensor_tensor(out=st[:, u, 4, :], in0=st[:, u, 3, :], scalar=D / 4.0,
                                                   in1=st[:, u, 4, :], op0=ALU.mult, op1=ALU.add))
                    dve.tensor_scalar(st[:, u, 0, :], st[:, u, 4, :], 1.0 / D, EPS,
                                      ALU.mult, ALU.add).then_inc(s_var, 1)
                for u in range(U):
                    n = it * U + u
                    dve.wait_ge(s_rstd, n + 1)
                    if u == 0:
                        dve.wait_ge(p_x2T, it * U + U)
                    for t in range(T):
                        last = dve.tensor_scalar(xn[:, u, D * t:D * t + D], seq[:, u, D * t:D * t + D],
                                                 st[:, u, 5, t:t + 1], st[:, u, 1, t:t + 1],
                                                 ALU.subtract, ALU.mult)
                    last.then_inc(s_xn, 1)
                for u in range(U):
                    n = it * U + u
                    dve.wait_ge(p_V, n + 1)
                    dve.tensor_tensor(tiles(V, u), lo[u][:, :].rearrange("p (t f) -> p t f", f=D), bv_b,
                                      ALU.add).then_inc(s_V, 1)
                for u in range(U):
                    n = it * U + u
                    dve.wait_ge(s_xn, n + 1)
                    xg = tiles(att, u)
                    dve.wait_ge(p_PT, n + 1)
                    chain(dve.tensor_tensor(xg, tiles(xn, u), g_b, ALU.mult))
                    chain(dve.tensor_reduce(st[:, u, 6, :], xg, AX.X, ALU.add))
                    chain(dve.tensor_scalar(st[:, u, 6, :], st[:, u, 6, :], bsum[:, :], 0.0,
                                            ALU.add, ALU.not_equal))
                    nat = st[:, u, 6, :].rearrange("p (j h) -> p j h", h=2)
                    scl = st[:, u, 9, :].rearrange("p (j s) -> p j s", s=2)
                    for h in range(2):
                        for s in range(2):
                            last = dve.tensor_copy(scl[D * h:D * h + D, :, s], nat[D * s:D * s + D, :, h])
                    last.then_inc(s_qm, 1)

                    dve.wait_ge(p_S, n + 1)
                    sc = lo[u][:, :].rearrange("p (t k) -> p t k", k=D)
                    a = tiles(att, u)
                    dve.scalar_tensor_tensor(out=a, in0=sc, scalar=NEG, in1=causal_b,
                                             op0=ALU.max, op1=ALU.min).then_inc(s_S, 1)
                    dve.wait_ge(s_S, n + 1)
                    dve.tensor_reduce(st[:, u, 2, :], a, AX.X, ALU.max).then_inc(s_max, 1)
                    dve.wait_ge(s_max, n + 1)
                    dve.tensor_tensor(a, a, spread(st[:, u, 2, :]), ALU.subtract).then_inc(s_sub, 1)
                for u in range(U):
                    n = it * U + u
                    a = tiles(att, u)
                    dve.wait_ge(s_exp, n + 1)
                    dve.tensor_reduce(st[:, u, 3, :], a, AX.X, ALU.add).then_inc(s_sum, 1)
                    dve.wait_ge(s_sum, n + 1)
                    chain(dve.reciprocal(st[:, u, 4, :], st[:, u, 3, :]))
                    dve.wait_ge(s_qm, n + 1)
                    dve.tensor_tensor(st[:, u, 4, :], st[:, u, 4, :], st[:, u, 9, :], ALU.mult).then_inc(s_inv, 1)
                    dve.wait_ge(s_inv, n + 1)
                    dve.tensor_tensor(a, a, spread(st[:, u, 4, :]), ALU.mult).then_inc(s_P, 1)
                for u in range(U):
                    n = it * U + u
                    dve.wait_ge(s_sq, n + 1)
                    dve.tensor_reduce(st[:, u, 5, :], tiles(xn, u), AX.X, ALU.add).then_inc(s_ss, 1)
                    dve.wait_ge(s_ss, n + 1)
                    dve.tensor_scalar(st[:, u, 7, :], st[:, u, 5, :], 1.0 / D, EPS, ALU.mult,
                                      ALU.add).then_inc(s_var2, 1)
                for u in range(U):
                    n = it * U + u
                    dve.wait_ge(s_rstd2, n + 1)
                    dve.tensor_tensor(tiles(xn, u), lo[u][:, :].rearrange("p (t f) -> p t f", f=D),
                                      spread(st[:, u, 8, :]), ALU.mult).then_inc(s_zn, 1)
                for u in range(U):
                    n = it * U + u
                    dve.wait_ge(p_Y, n + 1)
                    dve.scalar_tensor_tensor(out=seq2T[:, u, :], in0=hi[u][:, :], scalar=v1(B20),
                                             in1=x2T[:, u, :], op0=ALU.add, op1=ALU.add).then_inc(s_seq2T, 1)
                dve.wait_ge(s_seq2T, it * U + U)
                cols = seq2T[:, :, :].rearrange("p u (c q) -> p u c q", q=D)[:, :, :, D - 1]
                dve.tensor_tensor(xl[:, 0, :].rearrange("p (u c) -> p u c", u=U), cols,
                                  mlast[:, bass.ds(it * LC, LC)].rearrange("p (u c) -> p u c", u=U),
                                  ALU.mult).then_inc(c_last, 1)
                for u in range(U):
                    n = it * U + u
                    dve.wait_ge(p_seq2, n + 1)
                    m = mask[:, bass.ds(n * T, T)]
                    dve.tensor_tensor(tiles(seq2, u), lo[u][:, :].rearrange("p (t f) -> p t f", f=D),
                                      spread(m), ALU.mult).then_inc(s_seq2, 1)
                dve.wait_ge(c_pc, it + 1)
                dve.tensor_copy(xl[:, 1, :], hi[0][:, 0:LC]).then_inc(c_cen, 1)
                dve.wait_ge(c_pv, it + 1)
                dve.tensor_scalar(xl[:, 3, :], lo[0][:, 0:LC], EPS, None, ALU.add).then_inc(c_var, 1)
                for u in range(U):
                    dve.wait_ge(s_seq2, it * U + u + 1)
                    chain(dve.tensor_reduce(st[:, u, 6, :], tiles(seq2, u), AX.X, ALU.add))
                    dve.tensor_scalar(koff2[:, u * T:u * T + T], st[:, u, 6, :], 0.0, KEY_OFF,
                                      ALU.is_equal, ALU.mult).then_inc(s_koff2, 1)
                dve.wait_ge(c_rstd, it + 1)
                dve.tensor_tensor(xl[:, 5, :], xl[:, 1, :], xl[:, 4, :], ALU.mult).then_inc(c_xn, 1)
                dve.wait_ge(c_pS, it + 1)
                dve.scalar_tensor_tensor(out=s2[:, :], in0=hi[2][:, :], scalar=NEG, in1=diag2[:, :],
                                         op0=ALU.max, op1=ALU.min).then_inc(c_S, 1)
                dve.wait_ge(c_S, it + 1)
                dve.tensor_reduce(s2v[:, 0:1], s2[:, :], AX.X, ALU.max).then_inc(c_dve, 1)
                dve.wait_ge(c_dve, it * 4 + 1)
                dve.tensor_scalar(s2[:, :], s2[:, :], s2v[:, 0:1], None, ALU.subtract).then_inc(c_dve, 1)
                dve.wait_ge(c_exp, it + 1)
                dve.tensor_reduce(s2v[:, 1:2], s2[:, :], AX.X, ALU.add).then_inc(c_dve, 1)
                dve.wait_ge(c_dve, it * 4 + 3)
                dve.reciprocal(s2v[:, 2:3], s2v[:, 1:2]).then_inc(c_dve, 1)
                dve.wait_ge(c_dve, it * 4 + 4)
                dve.tensor_scalar(s2[:, :], s2[:, :], s2v[:, 2:3], None, ALU.mult).then_inc(c_P, 1)
                dve.wait_ge(c_pO, it + 1)
                dve.tensor_copy(o2[:, :], hi[3][:, 0:P]).then_inc(c_O, 1)

            CHAIN = U * (1 + 1 + 1 + 1 + 3 + 1 + 1)
            with dve.Fori(0, STEPS) as it:
                loop(it)

            def own(ins, k=[0]):
                k[0] += 1
                ins.then_inc(e_dve, 1)
                dve.wait_ge(e_dve, k[0])

            def rsqrt():
                own(dve.reciprocal(zr, zr))
                own(dve.tensor_tensor(zt, zv, zr, ALU.mult))
                own(dve.tensor_tensor(zt, zt, zr, ALU.mult))
                own(dve.tensor_scalar(zt, zt, -0.5, 1.5, ALU.mult, ALU.add))
                own(dve.tensor_tensor(zr, zr, zt, ALU.mult))

            dve.wait_ge(c_OT, STEPS + 1)
            dve.drain().then_inc(e_go, 1)
            dve.wait_ge(e_pe, 2)
            own(dve.tensor_scalar(qml, hi[1][:, 0:QL], 0.0, None, ALU.not_equal))
            own(dve.scalar_tensor_tensor(out=za, in0=hi[0][:, 0:QL], scalar=v1(BV1), in1=qml,
                                         op0=ALU.add, op1=ALU.mult))
            own(dve.tensor_tensor(za, za, XL[:, :], ALU.add))
            dve.wait_ge(e_pe, 3)
            own(dve.tensor_copy(zc, lo[0][:, 0:QL]))
            dve.wait_ge(e_pe, 4)
            dve.tensor_scalar(zv, lo[1][:, 0:QL], EPS, None, ALU.add).then_inc(e_var, 1)
            dve.wait_ge(e_act, 2)
            rsqrt()
            own(dve.tensor_tensor(zn, zc, zr, ALU.mult))
            dve.wait_ge(e_act, 3)
            dve.wait_ge(e_pe, 6)
            own(dve.scalar_tensor_tensor(out=zy, in0=lo[3][:, 0:QL], scalar=v1(B21), in1=zx,
                                         op0=ALU.add, op1=ALU.add))
            own(dve.tensor_tensor(zy, zy, mlast[:, :], ALU.mult))
            dve.wait_ge(e_pe, 7)
            own(dve.tensor_copy(zc, hi[2][:, 0:QL]))
            dve.wait_ge(e_pe, 8)
            dve.tensor_scalar(zv, hi[3][:, 0:QL], EPS, None, ALU.add).then_inc(e_var, 1)
            dve.wait_ge(e_act, 6)
            rsqrt()
            own(dve.tensor_tensor(zn, zc, zr, ALU.mult))
            dve.wait_ge(e_act, 7)
            ftv = FT.rearrange("p (g h s) -> p g h s", h=2, s=2)
            zxv = zx.rearrange("p (g s) -> p g s", s=2)
            for dup in range(2):
                for h in range(2):
                    own(dve.tensor_copy(ftv[D * dup:D * dup + D, :, h, :], zxv[D * h:D * h + D, :, :]))
            own(dve.tensor_copy(f_hi[:, :], FT))
            own(dve.tensor_tensor(FR, FT, f_hi[:, :], ALU.subtract))
            own(dve.tensor_copy(f_mid[:, :], FR))
            own(dve.tensor_copy(f_hl[0:D, :], f_hi[0:D, :]))
            dve.tensor_tensor(f_hl[D:P, :], FR[D:P, :], f_mid[D:P, :], ALU.subtract).then_inc(f_split, 1)

            def split(c, k, first=False):
                dve.wait_ge(i_hi, c + 1)
                dve.tensor_tensor(irem[k], it32[k], ihi[k][:, :], ALU.subtract).then_inc(i_rem, 1)
                dve.wait_ge(i_rem, c + 1)
                dve.tensor_copy(imid[k][:, :], irem[k]).then_inc(i_mid, 1)
                dve.wait_ge(i_mid, c + 1)
                if not first:
                    dve.wait_ge(i_mm, (c - 1) * (2 * NT))
                dve.tensor_copy(ix[k][0:D, :], ihi[k][0:D, :])
                dve.tensor_copy(ix[k][D:P, :], imid[k][D:P, :])
                dve.tensor_copy(iy[k][D:P, :], ihi[k][D:P, :])
                dve.tensor_tensor(iy[k][0:D, :], irem[k][0:D, :], imid[k][0:D, :],
                                  ALU.subtract).then_inc(i_xy, 1)

            def drain_even(c, k, free):
                if free is not None:
                    dve.wait_ge(o_st[k], free)
                for t in range(NT):
                    dve.wait_ge(i_mm, c * NT * 2 + 2 * t + 1)
                    dve.tensor_copy(ost[k * NT + t][:, 0:NB], banks[2 * t][:, 0:NB]).then_inc(o_even, 1)

            split(0, 0, True)
            split(1, 1, True)
            drain_even(0, 0, None)
            split(2, 0)
            drain_even(1, 1, None)
            with dve.Fori(1, CH // 2) as c2:
                split(c2 * 2 + 1, 1)
                drain_even(c2 * 2, 0, c2 * (16 * NT))
                split(c2 * 2 + 2, 0)
                drain_even(c2 * 2 + 1, 1, c2 * (16 * NT))
            drain_even(CH - 1, 0, (CH // 2) * (16 * NT))

        @block.scalar
        def _(act):
            def loop(it):
                for u in range(U):
                    n = it * U + u
                    act.wait_ge(p_seqT, n + 1)
                    act.activation(seqT[:, u, :], lo[u][:, :], ACT.Copy).then_inc(s_seqT, 1)
                for u in range(U):
                    n = it * U + u
                    act.wait_ge(p_K, n + 1)
                    act.activation(KT[:, u, :], hi[u][:, :], ACT.Identity, bias=v1(BK0)).then_inc(s_K, 1)
                for u in range(U):
                    n = it * U + u
                    if u == 0:
                        act.wait_ge(p_koff, it + 1)
                        act.activation(koffT[:, :], hi[0][0:U * T, 0:P], ACT.Copy).then_inc(s_koffT, 1)
                    act.wait_ge(p_xT, n + 1)
                    act.activation(xT[:, u, :], lo[u][:, :], ACT.Identity, bias=v1(LN1B0),
                                   scale=v1(LN1G0)).then_inc(s_xT, 1)
                for u in range(U):
                    n = it * U + u
                    act.wait_ge(p_Q, n + 1)
                    act.activation(QT[:, u, :], hi[u][:, :], ACT.Identity, bias=vec8[:, 0:1],
                                   scale=0.125).then_inc(s_Q, 1)
                for u in range(U):
                    n = it * U + u
                    act.wait_ge(s_sub, n + 1)
                    act.activation(att[:, u, :], att[:, u, :], ACT.Exp).then_inc(s_exp, 1)
                for u in range(U):
                    n = it * U + u
                    act.wait_ge(p_PT, n + 1 + U)
                    act.activation(PT[:, u, :], hi[u][:, :], ACT.Copy).then_inc(s_PT, 1)
                for u in range(U):
                    n = it * U + u
                    act.wait_ge(p_z, n + 1)
                    act.activation(xn[:, u, :], lo[u][:, :], ACT.Square).then_inc(s_sq, 1)
                for u in range(U):
                    n = it * U + u
                    act.wait_ge(p_x2T, n + 1 + U)
                    act.activation(x2T[:, u, :], hi[u][:, :], ACT.Identity, bias=v1(LN2B0),
                                   scale=v1(LN2G0)).then_inc(s_x2T, 1)
                for u in range(U):
                    n = it * U + u
                    act.wait_ge(p_H, n + 1)
                    act.activation(HT[:, u, :], lo[u][:, :], ACT.Relu, bias=v1(B10)).then_inc(s_H, 1)
                act.wait_ge(c_pc, it + 1)
                act.wait_ge(c_cen, it + 1)
                act.activation(xl[:, 2, :], hi[0][:, 0:LC], ACT.Square).then_inc(c_sq, 1)
                act.wait_ge(c_xn, it + 1)
                act.activation(XL[:, bass.ds(it * LC, LC)], xl[:, 5, :], ACT.Identity, bias=v1(LN1B1),
                               scale=v1(LN1G1)).then_inc(c_x, 1)
                act.activation(xl[:, 2, :], xl[:, 5, :], ACT.Identity, bias=v1(LN1B1),
                               scale=v1(LN1G1)).then_inc(c_x, 1)
                act.wait_ge(c_pk, it + 1)
                act.activation(koffT2[:, :], lo[2][0:U * T, 0:P], ACT.Copy).then_inc(c_kT, 1)
                act.wait_ge(c_pq, it + 1)
                for h in range(2):
                    a, b = D * h, D * h + D
                    act.activation(QB[a:b, :, 2 * J * h:2 * J * h + 2 * J],
                                   hi[1][a:b, 0:LC].rearrange("p (u c) -> p u c", u=U), ACT.Identity,
                                   bias=vec8[a:b, 1:2], scale=0.125).then_inc(c_QB, 1)
                act.wait_ge(c_pa, it + 1)
                act.activation(AB[:, :, :].rearrange("p u c -> p (u c)"), lo[1][:, 0:P],
                               ACT.Copy).then_inc(c_AB, 1)
                act.wait_ge(c_dve, it * 4 + 2)
                act.activation(s2[:, :], s2[:, :], ACT.Exp).then_inc(c_exp, 1)
                act.wait_ge(c_pPT, it + 1)
                act.activation(PT2[:, :], lo[3][:, :], ACT.Copy).then_inc(c_PT, 1)
                act.wait_ge(c_pOT, it + 1)
                src = hi[0][:, 0:P].rearrange("p (u m) -> p u m", u=U)
                for h in range(2):
                    a, b = D * h, D * h + D
                    last = act.activation(OT[a:b, bass.ds(it * LC, LC)].rearrange("p (u c) -> p u c", u=U),
                                          src[a:b, :, 2 * J * h:2 * J * h + 2 * J], ACT.Copy)
                last.then_inc(c_OT, 1)

            act.sem_inc(c_OT, 1)
            with act.Fori(0, STEPS) as it:
                loop(it)

            act.wait_ge(e_dve, 4)
            act.activation(zs, lo[0][:, 0:QL], ACT.Square).then_inc(e_act, 1)
            act.wait_ge(e_var, 1)
            act.activation(zr, zv, ACT.Sqrt).then_inc(e_act, 1)
            act.wait_ge(e_dve, 10)
            act.activation(zx, zn, ACT.Identity, bias=v1(LN2B1), scale=v1(LN2G1)).then_inc(e_act, 1)
            act.wait_ge(e_pe, 5)
            act.activation(zh, lo[2][:, 0:QL], ACT.Relu, bias=v1(B11)).then_inc(e_act, 1)
            act.wait_ge(e_dve, 13)
            act.activation(zs, hi[2][:, 0:QL], ACT.Square).then_inc(e_act, 1)
            act.wait_ge(e_var, 2)
            act.activation(zr, zv, ACT.Sqrt).then_inc(e_act, 1)
            act.wait_ge(e_dve, 19)
            act.activation(zx, zn, ACT.Identity, bias=v1(LNFB), scale=v1(LNFG)).then_inc(e_act, 1)

            def high(c, k, c2, freed=None):
                act.wait_ge(i_load[k], c2 * 32 + 32)
                if freed is not None:
                    act.wait_ge(i_xy, freed)
                act.activation(ihi[k][:, :], it32[k], ACT.Copy).then_inc(i_hi, 1)

            def drain_odd(c, k, free):
                if free is not None:
                    act.wait_ge(o_st[k], free)
                for t in range(NT):
                    act.wait_ge(i_mm, c * NT * 2 + 2 * t + 2)
                    act.activation(ost[k * NT + t][:, NB:NC], banks[2 * t + 1][:, 0:NB],
                                   ACT.Copy).then_inc(o_odd, 1)

            high(0, 0, 0)
            high(1, 1, 0)
            high(2, 0, 1, 1)
            drain_odd(0, 0, None)
            high(3, 1, 1, 2)
            drain_odd(1, 1, None)
            with act.Fori(1, CH // 2 - 1) as c2:
                high(c2 * 2 + 2, 0, c2 + 1, c2 * 2 + 1)
                drain_odd(c2 * 2, 0, c2 * (16 * NT))
                high(c2 * 2 + 3, 1, c2 + 1, c2 * 2 + 2)
                drain_odd(c2 * 2 + 1, 1, c2 * (16 * NT))
            high(CH - 1, 0, CH // 2, CH - 2)
            drain_odd(CH - 3, 0, (CH // 2 - 1) * (16 * NT))
            drain_odd(CH - 2, 1, (CH // 2 - 1) * (16 * NT))
            drain_odd(CH - 1, 0, (CH // 2) * (16 * NT))

        @block.tensor
        def _(pe):
            def mm(o, l, r, start=True):
                return pe.matmul(o, l, r, start=start, stop=True, skip_group_check=True)

            def turn(bank, src):
                for j in range(J):
                    last = pe.transpose(bank[:, P * j:P * j + P], src[:, P * j:P * j + P], ident[:, :])
                return last

            pe.sem_inc(p_x2T, U)
            pe.sem_inc(p_PT, U)
            pe.wait_ge(s_prep, n_prep[0])
            pe.wait_ge(s_const, n_const[0])

            def loop(it):
                pe.wait_ge(c_OT, it + 1)
                for u in range(U):
                    n = it * U + u
                    pe.wait_ge(s_seq, n + 1)
                    turn(lo[u], seq[:, u, :]).then_inc(p_seqT, 1)
                for u in range(U):
                    n = it * U + u
                    pe.wait_ge(s_seqT, n + 1)
                    mm(hi[u][:, :], wbd[:, WK0, :], seqT[:, u, :]).then_inc(p_K, 1)
                for u in range(U):
                    n = it * U + u
                    for j in range(J):
                        last = mm(lo[u][:, P * j:P * j + P], seqT[:, u, P * j:P * j + P], wbd[:, WV0, :], j == 0)
                    last.then_inc(p_V, 1)
                pe.wait_ge(s_K, it * U + 1)
                pe.wait_ge(s_koff, (it * U + U) * 2)
                pe.transpose(hi[0][0:U * T, 0:P], koff[:, :], ident[:, :]).then_inc(p_koff, 1)
                for u in range(U):
                    n = it * U + u
                    pe.wait_ge(s_V, n + 1)
                    pe.wait_ge(s_xn, n + 1)
                    turn(lo[u], xn[:, u, :]).then_inc(p_xT, 1)
                for u in range(U):
                    n = it * U + u
                    pe.wait_ge(s_xT, n + 1)
                    pe.wait_ge(s_K, n + 1)
                    pe.wait_ge(s_koffT, it + 1)
                    mm(hi[u][:, :], wbd[:, WQ0, :], xT[:, u, :]).then_inc(p_Q, 1)
                for u in range(U):
                    n = it * U + u
                    pe.wait_ge(s_Q, n + 1)
                    for j in range(J):
                        mm(lo[u][:, P * j:P * j + P], sel1[:, (u * J + j) * P:(u * J + j) * P + P],
                           koffT[:, :], j == 0)
                    for h in range(2):
                        a, b = D * h, D * h + D
                        for c in range(T):
                            last = mm(lo[u][a:b, D * c:D * c + D], QT[a:b, u, D * c:D * c + D],
                                      KT[a:b, u, D * c:D * c + D], False)
                    last.then_inc(p_S, 1)
                for u in range(U):
                    n = it * U + u
                    pe.wait_ge(s_P, n + 1)
                    turn(hi[u], att[:, u, :]).then_inc(p_PT, 1)
                for u in range(U):
                    n = it * U + u
                    pe.wait_ge(s_PT, n + 1)
                    for j in range(J):
                        mm(lo[u][:, P * j:P * j + P], xT[:, u, P * j:P * j + P], center[:, :], j == 0)
                    for s in range(2):
                        a, b = D * s, D * s + D
                        for j in range(J):
                            for h in range(2):
                                t = 2 * j + h
                                last = mm(lo[u][a:b, D * t:D * t + D], PT[a:b, u, D * t:D * t + D],
                                          V[a:b, u, D * t:D * t + D], False)
                    last.then_inc(p_z, 1)
                for u in range(U):
                    n = it * U + u
                    pe.wait_ge(s_zn, n + 1)
                    turn(hi[u], xn[:, u, :]).then_inc(p_x2T, 1)
                for u in range(U):
                    n = it * U + u
                    pe.wait_ge(s_x2T, n + 1)
                    mm(lo[u][:, :], wbd[:, W10, :], x2T[:, u, :]).then_inc(p_H, 1)
                for u in range(U):
                    n = it * U + u
                    pe.wait_ge(s_H, n + 1)
                    mm(hi[u][:, :], wbd[:, W20, :], HT[:, u, :]).then_inc(p_Y, 1)
                for u in range(U):
                    n = it * U + u
                    pe.wait_ge(s_seq2T, n + 1)
                    turn(lo[u], seq2T[:, u, :]).then_inc(p_seq2, 1)
                pe.wait_ge(c_last, it + 1)
                mm(hi[0][:, 0:LC], center[:, :], xl[:, 0, :]).then_inc(c_pc, 1)
                pe.wait_ge(c_sq, it + 1)
                pe.wait_ge(s_seq2, it * U + U)
                mm(lo[0][:, 0:LC], mean_m[:, :], xl[:, 2, :]).then_inc(c_pv, 1)
                pe.wait_ge(s_koff2, it * U + U)
                pe.transpose(lo[2][0:U * T, 0:P], koff2[:, :], ident[:, :]).then_inc(c_pk, 1)
                pe.wait_ge(c_x, it * 2 + 2)
                mm(hi[1][:, 0:LC], wbd[:, WQ1, :], xl[:, 2, :]).then_inc(c_pq, 1)
                pe.wait_ge(c_kT, it + 1)
                for j in range(J):
                    mm(hi[2][:, P * j:P * j + P], sel2[:, P * j:P * j + P], koffT2[:, :], j == 0)
                pe.wait_ge(c_QB, it * 2 + 2)
                QBf = QB[:, :, :].rearrange("p u c -> p (u c)")
                mm(lo[1][:, 0:P], wbd[:, WKT1, :], QBf).then_inc(c_pa, 1)
                mm(hi[2][:, :], QBf, bkrep[:, :], False)
                pe.wait_ge(c_AB, it + 1)
                for u in range(U):
                    last = mm(hi[2][ROWS * u:ROWS * u + ROWS, :], AB[:, u, :], seq2T[:, u, :], False)
                last.then_inc(c_pS, 1)
                pe.wait_ge(c_P, it + 1)
                turn(lo[3], s2[:, :]).then_inc(c_pPT, 1)
                pe.wait_ge(c_PT, it + 1)
                for u in range(U):
                    for j in range(J):
                        last = mm(hi[3][ROWS * u:ROWS * u + ROWS, 0:P],
                                  PT2[:, P * j + ROWS * u:P * j + ROWS * u + ROWS],
                                  seq2[:, u, P * j:P * j + P], j == 0)
                last.then_inc(c_pO, 1)
                pe.wait_ge(c_O, it + 1)
                pe.transpose(hi[0][:, 0:P], o2[:, :], ident[:, :]).then_inc(c_pOT, 1)

            with pe.Fori(0, STEPS) as it:
                loop(it)

            pe.wait_ge(c_OT, STEPS + 1)
            mm(hi[0][:, 0:QL], wbd[:, WV1, :], OT[:, :]).then_inc(e_pe, 1)
            mm(hi[1][:, 0:QL], mean_m[:, :], XL[:, :]).then_inc(e_pe, 1)
            pe.wait_ge(e_dve, 3)
            mm(lo[0][:, 0:QL], center[:, :], za).then_inc(e_pe, 1)
            pe.wait_ge(e_act, 1)
            mm(lo[1][:, 0:QL], mean_m[:, :], zs).then_inc(e_pe, 1)
            pe.wait_ge(e_act, 3)
            mm(lo[2][:, 0:QL], wbd[:, W11, :], zx).then_inc(e_pe, 1)
            pe.wait_ge(e_act, 4)
            mm(lo[3][:, 0:QL], wbd[:, W21, :], zh).then_inc(e_pe, 1)
            pe.wait_ge(e_dve, 12)
            mm(hi[2][:, 0:QL], center[:, :], zy).then_inc(e_pe, 1)
            pe.wait_ge(e_act, 5)
            mm(hi[3][:, 0:QL], mean_m[:, :], zs).then_inc(e_pe, 1)

            pe.wait_ge(f_split, 1)

            def product(c, k, first):
                pe.wait_ge(i_xy, c + 1)
                for t in range(NT):
                    for half in range(2):
                        b = banks[2 * t + half]
                        if not first:
                            pe.wait_ge(o_even if half == 0 else o_odd, (c - 1) * NT + t + 1)
                        xs = ix[k][:, NB * half:NB * half + NB]
                        ys = iy[k][:, NB * half:NB * half + NB]
                        mm(b[:, 0:NB], f_hi[:, P * t:P * t + P], xs)
                        mm(b[:, 0:NB], f_mid[:, P * t:P * t + P], xs, False)
                        last = mm(b[:, 0:NB], f_hl[:, P * t:P * t + P], ys, False)
                        last.then_inc(i_mm, 1)

            product(0, 0, True)
            with pe.Fori(0, CH // 2) as c2:
                product(c2 * 2 + 1, 1, False)
                product(c2 * 2 + 2, 0, False)



def kernel(r_input_ids, L0_rec_item_emb, L0_rec_pos_emb, L0_rec_ln1_g, L0_rec_ln1_b, L0_rec_Wq, L0_rec_bq,
           L0_rec_Wk, L0_rec_bk, L0_rec_Wv, L0_rec_bv, L0_rec_ln2_g, L0_rec_ln2_b, L0_rec_W1, L0_rec_b1,
           L0_rec_W2, L0_rec_b2, L0_rec_lnf_g, L0_rec_lnf_b, L0_rec_out_item_emb):
    import numpy as np
    import concourse.bacc as bacc
    from concourse.bass_utils import run_bass_kernel_spmd

    a = lambda x: np.ascontiguousarray(x)
    ids = np.asarray(r_input_ids)
    nb = ids.shape[0]
    groups = nb // (2 * T)
    g1, b1_, bq, bk, bv = (np.asarray(x) for x in (L0_rec_ln1_g, L0_rec_ln1_b, L0_rec_bq, L0_rec_bk, L0_rec_bv))
    g2, b2_, f1, f2 = (np.asarray(x) for x in (L0_rec_ln2_g, L0_rec_ln2_b, L0_rec_b1, L0_rec_b2))
    wq, wk, wv, w1, w2 = (np.asarray(x) for x in (L0_rec_Wq, L0_rec_Wk, L0_rec_Wv, L0_rec_W1, L0_rec_W2))
    vec_list = [g1[0], b1_[0], bq[0], bk[0], g2[0], b2_[0], f1[0], f2[0],
                g1[1], b1_[1], bq[1], bv[1], g2[1], b2_[1], f1[1], f2[1],
                np.asarray(L0_rec_lnf_g), np.asarray(L0_rec_lnf_b), bk[1]]
    w_list = [wq[0], wk[0], wv[0], w1[0], w2[0], wq[1], wk[1].T, wv[1], w1[1], w2[1]]

    f = np.float32
    eye = np.eye(P, dtype=f)
    blocks = np.kron(np.eye(2, dtype=f), np.ones((D, D), f))
    q = np.arange(P) % D
    causal = np.where(np.arange(D)[None, :] <= q[:, None], f(3e38), f(NEG)).astype(f)
    sel1 = np.zeros((U, T, U, J, 2, D), f)
    sel2 = np.zeros((U, T, J, U, ROWS), f)
    diag2 = np.full((U, ROWS, J, 2, D), f(3e38), f)
    for u in range(U):
        for j in range(J):
            for h in range(2):
                sel1[u, 2 * j + h, u, j, h, :] = 1
                for jj in range(J):
                    for s in range(2):
                        m = (h * J + jj) * 2 + s
                        sel2[u, 2 * j + h, j, u, m] = 1
                        if (jj, s) != (j, 0):
                            diag2[u, m, j, 0, :] = -1e38
                        if (jj, s) != (j, 1):
                            diag2[u, m, j, 1, :] = -1e38
    arrays = {
        "ids_tok": a(ids.reshape(-1, P).T),
        "ids_last": a(ids[:, -1].reshape(groups, J, 2, 2).transpose(2, 0, 1, 3).reshape(2, -1)),
        "item_emb": a(L0_rec_item_emb),
        "vecs": a(np.stack(vec_list, 1)),
        "weights": a(np.stack(w_list, 1)),
        "pos": a(L0_rec_pos_emb),
        "bv_row": a(bv[0:1]),
        "g_row": a(g1[0:1]),
        "b_row": a(b1_[0:1]),
        "items_t": a(np.asarray(L0_rec_out_item_emb).T),
        "ident_c": eye,
        "center_c": (eye - blocks / D).astype(f),
        "mean_c": (blocks / D).astype(f),
        "causal_c": causal,
        "diag2_c": diag2.reshape(P, W),
        "sel1_c": sel1.reshape(U * T, -1),
        "sel2_c": sel2.reshape(U * T, -1),
    }
    nc = bacc.Bacc("TRN2", target_bir_lowering=False, num_devices=1)
    args = [nc.dram_tensor(k, v.shape, mybir.dt.from_np(v.dtype), kind="ExternalInput").ap()
            for k, v in arrays.items()]
    out = nc.dram_tensor("scores_out", (nb, L0_rec_out_item_emb.shape[0]), F32, kind="ExternalOutput").ap()
    build(nc, *args, out)
    r = run_bass_kernel_spmd(nc, [arrays], core_ids=[0])
    return r.results[0]["scores_out"]
```

```python
from contextlib import ExitStack

import concourse.bass as bass
from concourse import mybir

F32 = mybir.dt.float32
BF16 = mybir.dt.bfloat16
I32 = mybir.dt.int32
ALU = mybir.AluOpType
ACT = mybir.ActivationFunctionType
AX = mybir.AxisListType

P = 128
D = 64
EPS = 0.001
NEG = -2.0 ** 32
KEY_OFF = -2.0 ** 100
U = 4
J = 4
W = J * P
T = 2 * J
RSQRT_MAGIC = float(0x5F3759DF)
(VAR, RSTD, TMP, SUM, DIF, MEAN, NMAX, ESUM, INV, XSUM, QMASK, SQ, VAR2, RSTD2, TMP2, KSUM, NST) = range(17)
ROWS = 32

(LN1G0, LN1B0, BQ0, BK0, LN2G0, LN2B0, B10, B20,
 LN1G1, LN1B1, BQ1, BV1, LN2G1, LN2B1, B11, B21, LNFG, LNFB, BK1, NVEC) = range(20)
WQ0, WK0, WV0, W10, W20, WQ1, WKT1, WV1, W11, W21, NW = range(11)


def build(nc, ids_tok, ids_last, item_emb, vecs, weights, pos, bv_row, ln_rows, items_t,
          ident_c, center_c, mean_c, causal_c, diag2_c, sel1_c, sel2_c, out):
    n_tiles = ids_tok.shape[1]
    STEPS = n_tiles // (U * T)
    NITEMS = items_t.shape[1]
    B = out.shape[0]
    NROW = item_emb.shape[0]
    QL = B // 2
    LC = U * J * 2

    with ExitStack() as ctx:
        def sb(name, shape, dt=F32):
            return ctx.enter_context(nc.sbuf_tensor(name, shape, dt))

        def sem(name):
            return ctx.enter_context(nc.semaphore(name))

        banks = [ctx.enter_context(nc.psum_tensor(f"bank{i}", [P, 512], F32)) for i in range(8)]
        lo, hi = banks[:4], banks[4:]
        front = banks[:4]
        spare = banks[7]

        def back(stage, u):
            if stage == 0:
                return banks[4 + u]
            return banks[4 + ((stage - 1) * U + u) % 3]

        ident = sb("ident", [P, P])
        center = sb("center", [P, P])
        mean_m = sb("mean_m", [P, P])
        causal = sb("causal", [P, D])
        diag2 = sb("diag2", [P, W])
        sel1 = sb("sel1", [U * T, U * J * P], BF16)
        sel2 = sb("sel2", [U * T, J * P], BF16)
        vec = sb("vec", [P, NVEC])
        vec8 = sb("vec8", [P, 2])
        wbd = sb("wbd", [P, NW, P])
        wmean = sb("wmean", [P, 5])
        pos2 = sb("pos2", [P, D])
        bvr = sb("bvr", [P, D])
        gain_row = sb("gain_row", [P, D])
        bias_row = sb("bias_row", [P, D])
        bv3 = sb("bv3", [P, 3, D], BF16)
        bv_rows = sb("bv_rows", [P, W], BF16)
        ones3 = sb("ones3", [3, P], BF16)
        bkrep = sb("bkrep", [P, W])
        ids_i = sb("ids_i", [P, n_tiles], I32)
        ids_f = sb("ids_f", [P, n_tiles])
        ids_n = sb("ids_n", [P, n_tiles])
        idx = sb("idx", [P, n_tiles], I32)
        idx_now = sb("idx_now", [P, U * T], I32)
        mask = sb("mask", [P, n_tiles])
        idl_i = sb("idl_i", [P, QL], I32)
        mlast = sb("mlast", [P, QL])

        emb = sb("emb", [P, U, W])
        seq = sb("seq", [P, U, W])
        seqT = sb("seqT", [P, U, W])
        KT = sb("KT", [P, U, W])
        V = sb("V", [P, U, W])
        xn = sb("xn", [P, U, W])
        xT = sb("xT", [P, U, W])
        QT = sb("QT", [P, U, W])
        att = sb("att", [P, U, W])
        PT = sb("PT", [P, U, W])
        zq = sb("zq", [P, U, W])
        zn_ = sb("zn", [P, U, W])
        xg = sb("xg", [P, U, W])
        sel1f = zq[0:U * T, :, :].rearrange("p u w -> p (u w)")
        sel2f = zn_[0:U * T, 0, :]
        x2T = sb("x2T", [P, U, W])
        HT = sb("HT", [P, U, W])
        seq2T = sb("seq2T", [P, U, W])
        seq2 = sb("seq2", [P, U, W])
        stat = sb("stat", [P, U, T, 6])
        st = sb("st", [P, NST, U, T])
        koff = sb("koff", [P, U * T])
        koffT = sb("koffT", [U * T, P], BF16)
        koff2 = sb("koff2", [P, U * T])
        koffT2 = sb("koffT2", [U * T, P], BF16)

        xl = sb("xl", [P, 8, LC])
        QB = sb("QB", [P, U, ROWS])
        AB = sb("AB", [P, U, ROWS])
        s2 = sb("s2", [P, W])
        s2v = sb("s2v", [P, 4])
        PT2 = sb("PT2", [P, W])
        o2 = sb("o2", [P, P])
        XL = sb("XL", [P, QL])
        OT = sb("OT", [P, QL])

        s_const = sem("s_const")
        s_ids = sem("s_ids")
        s_zero = sem("s_zero")
        s_prep = sem("s_prep")
        s_idx = sem("s_idx")
        s_now = sem("s_now")
        s_gath = [sem(f"s_gath{u}") for u in range(U)]
        s_room = sem("s_room")
        s_raw = sem("s_raw")
        s_seq = sem("s_seq")
        s_stat = sem("s_stat")
        s_pre = sem("s_pre")
        s_m2 = sem("s_m2")
        s_mean = sem("s_mean")
        s_shift = sem("s_shift")
        s_koff = sem("s_koff")
        s_xn = sem("s_xn")
        s_xg = sem("s_xg")
        s_xsum = sem("s_xsum")
        s_qm = sem("s_qm")
        p_seqT = sem("p_seqT")
        s_seqT = sem("s_seqT")
        p_K = sem("p_K")
        s_K = sem("s_K")
        p_V = sem("p_V")
        s_V = sem("s_V")
        p_koff = sem("p_koff")
        s_koffT = sem("s_koffT")
        p_xT = sem("p_xT")
        s_xT = sem("s_xT")
        p_Q = sem("p_Q")
        s_Q = sem("s_Q")
        p_S = sem("p_S")
        s_S = sem("s_S")
        s_max = sem("s_max")
        s_exp = sem("s_exp")
        s_rec = sem("s_rec")
        s_inv = sem("s_inv")
        s_P = sem("s_P")
        p_PT = sem("p_PT")
        s_PT = sem("s_PT")
        p_z = sem("p_z")
        s_sq = sem("s_sq")
        s_ss = sem("s_ss")
        s_var2 = sem("s_var2")
        s_zn = sem("s_zn")
        p_x2T = sem("p_x2T")
        s_x2T = sem("s_x2T")
        p_H = sem("p_H")
        s_H = sem("s_H")
        p_Y = sem("p_Y")
        s_seq2T = sem("s_seq2T")
        p_seq2 = sem("p_seq2")
        s_seq2 = sem("s_seq2")
        s_ksum2 = sem("s_ksum2")
        s_koff2 = sem("s_koff2")
        c_last = sem("c_last")
        c_pc = sem("c_pc")
        c_cen = sem("c_cen")
        c_sq = sem("c_sq")
        c_pv = sem("c_pv")
        c_var = sem("c_var")
        c_xn = sem("c_xn")
        c_x = sem("c_x")
        c_XL = sem("c_XL")
        c_pq = sem("c_pq")
        c_QB = sem("c_QB")
        c_pa = sem("c_pa")
        c_AB = sem("c_AB")
        c_pk = sem("c_pk")
        c_kT = sem("c_kT")
        c_pS = sem("c_pS")
        c_S = sem("c_S")
        c_max = sem("c_max")
        c_inv = sem("c_inv")
        c_exp = sem("c_exp")
        c_P = sem("c_P")
        c_pPT = sem("c_pPT")
        c_PT = sem("c_PT")
        c_pO = sem("c_pO")
        c_O = sem("c_O")
        c_pOT = sem("c_pOT")
        c_OT = sem("c_OT")

        za = seq[:, 0, 0:QL]
        zc = seq[:, 1, 0:QL]
        zs = seq[:, 2, 0:QL]
        zv = seq[:, 3, 0:QL]
        zr = xn[:, 0, 0:QL]
        zn = xn[:, 1, 0:QL]
        zx = xn[:, 2, 0:QL]
        zh = xn[:, 3, 0:QL]
        zy = att[:, 0, 0:QL]
        zt = x2T[:, 0, 0:QL]
        qml = att[:, 1, 0:QL]
        FT = att[:, 2, :]
        FR = att[:, 3, :]
        FM = PT[:, 0, :]
        f_hi = sb("f_hi", [P, B], BF16)
        f_mid = sb("f_mid", [P, B], BF16)
        f_hl = sb("f_hl", [P, B], BF16)
        NB = 500
        NC = 1000
        CH = NITEMS // NC
        NT = B // P
        it32 = [emb[0:D, 2 * i:2 * i + 2, :].rearrange("p a b -> p (a b)")[:, 0:NC] for i in range(2)]
        irem = xg[0:D, 0:2, :].rearrange("p a b -> p (a b)")[:, 0:NC]
        imid = sb("imid", [D, NC], BF16)
        SLOTS = 4
        ix = [sb(f"ix{i}", [P, NC], BF16) for i in range(SLOTS)]
        iy = [sb(f"iy{i}", [P, NC], BF16) for i in range(SLOTS)]
        AHEAD = 3
        FIRST = 2
        ROUNDS = (CH - FIRST - AHEAD) // SLOTS
        assert CH * NC == NITEMS and FIRST + AHEAD + ROUNDS * SLOTS == CH and CH % 2 == 1
        ost = [(KT, V, QT, HT)[i][:, 2 * k:2 * k + 2, :].rearrange("p a b -> p (a b)")[:, 0:NC]
               for k in range(2) for i in range(4)]
        e_go = sem("e_go")
        e_pe = sem("e_pe")
        e_dve = sem("e_dve")
        e_act = sem("e_act")
        e_var = sem("e_var")
        f_split = sem("f_split")
        i_load = [sem(f"i_load{i}") for i in range(2)]
        i_hi = sem("i_hi")
        i_rem = sem("i_rem")
        i_mid = sem("i_mid")
        i_hs = sem("i_hs")
        i_xy = sem("i_xy")
        i_mm = sem("i_mm")
        o_even = sem("o_even")
        o_odd = sem("o_odd")
        o_st = [sem(f"o_st{i}") for i in range(2)]

        block = ctx.enter_context(nc.Block())

        def v1(c, h=None):
            return vec[:, c:c + 1] if h is None else vec[D * h:D * h + D, c:c + 1]

        def tiles(buf, u):
            return buf[:, u, :].rearrange("p (t f) -> p t f", f=D)

        def spread(small):
            return small.unsqueeze(2).broadcast_to([P, T, D])

        n_const = [0]
        n_prep = [0]

        @block.sync
        def _(sp):
            def load(dst, src):
                sp.dma_start(dst, src).then_inc(s_const, 16)
                n_const[0] += 16
            sp.dma_start(ids_i[:, :], ids_tok).then_inc(s_ids, 16)
            for h in range(2):
                load(idl_i[D * h:D * h + D, :], ids_last[h:h + 1, :].broadcast_to([D, QL]))
            load(ident[:, :], ident_c)
            load(center[:, :], center_c)
            load(mean_m[:, :], mean_c)
            load(causal[:, :], causal_c)
            load(diag2[:, :], diag2_c)
            load(sel1f, sel1_c)
            load(sel2f, sel2_c)
            for h in range(2):
                load(vec[D * h:D * h + D, :], vecs)
                load(pos2[D * h:D * h + D, :], pos)
            load(bvr[:, :], bv_row.broadcast_to([P, D]))
            load(gain_row[:, :], ln_rows[0:1, :].broadcast_to([P, D]))
            load(bias_row[:, :], ln_rows[1:2, :].broadcast_to([P, D]))
            sp.wait_ge(s_zero, 1)
            for h in range(2):
                load(wbd[D * h:D * h + D, :, D * h:D * h + D], weights)

            def store(c, k):
                for t in range(NT):
                    sp.wait_ge(o_even, (c * NT + t) + 1)
                    sp.wait_ge(o_odd, (c * NT + t) + 1)
                    sp.dma_start(out[P * t:P * t + P, bass.ds(c * NC, NC)],
                                 ost[k * NT + t]).then_inc(o_st[k], 16)

            with sp.Fori(0, CH // 2) as c2:
                store(c2 * 2, 0)
                store(c2 * 2 + 1, 1)
            store(CH - 1, 0)
            for k in range(2):
                sp.wait_ge(o_st[k], 16 * NT * ((CH + 1 - k) // 2))

        @block.gpsimd
        def _(pool):
            pool.memset(wbd[:, :, :], 0.0).then_inc(s_zero, 1)
            pool.memset(QB[:, :, :], 0.0).then_inc(s_zero, 1)

            def gather(i, u):
                if u == 0:
                    if not isinstance(i, int) or i > 0:
                        for v in range(U):
                            pool.wait_ge(s_gath[v], i * (16 * T))
                    pool.tensor_copy(idx_now[:, :], idx[:, bass.ds(i * (U * T), U * T)]).then_inc(s_now, 1)
                    pool.wait_ge(s_now, i + 1)
                if not isinstance(i, int) or i > 0:
                    pool.wait_ge(s_raw, (i - 1) * U + u + 1)
                pool.sem_inc(s_room, 1)
                for t in range(T):
                    pool.indirect_dma_start(
                        out=emb[:, u, D * t:D * t + D], out_offset=None, in_=item_emb,
                        in_offset=bass.IndirectOffsetOnAxis(ap=idx_now[:, u * T + t:u * T + t + 1], axis=0),
                    ).then_inc(s_gath[u], 16)

            pool.wait_ge(s_idx, 1)
            pool.wait_ge(s_zero, 2)
            gain_b = gain_row[:, :].unsqueeze(1).broadcast_to([P, T, D])

            def gained(i):
                for u in range(U):
                    if not isinstance(i, int) or i > 0:
                        pool.wait_ge(s_xsum, (i - 1) * U + u + 1)
                    pool.wait_ge(s_xn, i * U + u + 1)
                    pool.tensor_tensor(tiles(xg, u), tiles(xn, u), gain_b, ALU.mult).then_inc(s_xg, 1)

            for u in range(U):
                gather(0, u)
            gather(1, 0)
            gather(1, 1)
            pool.wait_ge(s_const, n_const[0])
            gained(0)
            gather(1, 2)
            gather(1, 3)
            with pool.Fori(2, STEPS) as i:
                for u in range(U):
                    gather(i, u)
                gained(i - 1)
            gained(STEPS - 1)

            def load_items(c, k, first=False):
                if not first:
                    pool.wait_ge(i_hi, c - 1)
                    pool.wait_ge(i_rem, c - 1)
                pool.dma_start(it32[k], items_t[:, bass.ds(c * NC, NC)]).then_inc(i_load[k], 16)

            pool.wait_ge(s_raw, STEPS * U)
            load_items(0, 0, True)
            load_items(1, 1, True)
            with pool.Fori(1, CH // 2) as c2:
                load_items(c2 * 2, 0)
                load_items(c2 * 2 + 1, 1)
            load_items(CH - 1, 0)

        @block.vector
        def _(dve):
            step_no = n_prep

            def prep(ins):
                step_no[0] += 1
                ins.then_inc(s_prep, 1)
                dve.wait_ge(s_prep, step_no[0])

            dve.wait_ge(s_ids, 16)
            prep(dve.tensor_copy(ids_f[:, :], ids_i[:, :]))
            prep(dve.tensor_scalar(mask[:, :], ids_f[:, :], float(NROW - 1), None, ALU.not_equal))
            prep(dve.tensor_scalar(ids_n[:, :], ids_f[:, :], 0.0, float(NROW), ALU.is_lt, ALU.mult))
            prep(dve.tensor_tensor(ids_f[:, :], ids_f[:, :], ids_n[:, :], ALU.add))
            prep(dve.tensor_scalar(ids_f[:, :], ids_f[:, :], 0.0, float(NROW - 1), ALU.max, ALU.min))
            dve.tensor_copy(idx[:, :], ids_f[:, :]).then_inc(s_idx, 1)
            dve.wait_ge(s_const, n_const[0])
            prep(dve.tensor_scalar(mlast[:, :], idl_i[:, :], float(NROW - 1), None, ALU.not_equal))
            prep(dve.tensor_copy(sel1[:, :], sel1f))
            prep(dve.tensor_copy(sel2[:, :], sel2f))
            prep(dve.tensor_scalar(vec8[:, 0:1], v1(BQ0), 0.125, None, ALU.mult))
            prep(dve.tensor_scalar(vec8[:, 1:2], v1(BQ1), 0.125, None, ALU.mult))
            for h in range(2):
                a, b = D * h, D * h + D
                blk = wbd[a:b, WV0, a:b]
                prep(dve.tensor_reduce(wmean[a:b, 0:1], blk, AX.X, ALU.add))
                prep(dve.tensor_scalar(wmean[a:b, 1:2], wmean[a:b, 0:1], 1.0 / D, None, ALU.mult))
                prep(dve.tensor_scalar(blk, blk, wmean[a:b, 1:2], None, ALU.subtract))
            prep(dve.tensor_reduce(wmean[:, 4:5], bias_row[:, :], AX.X, ALU.add))
            prep(dve.tensor_reduce(wmean[:, 2:3], bvr[:, :], AX.X, ALU.add))
            prep(dve.tensor_scalar(wmean[:, 3:4], wmean[:, 2:3], 1.0 / D, None, ALU.mult))
            prep(dve.tensor_scalar(bvr[:, :], bvr[:, :], wmean[:, 3:4], None, ALU.subtract))
            prep(dve.tensor_copy(bv3[:, 0, :], bvr[:, :]))
            prep(dve.tensor_tensor(bvr[:, :], bvr[:, :], bv3[:, 0, :], ALU.subtract))
            prep(dve.tensor_copy(bv3[:, 1, :], bvr[:, :]))
            prep(dve.tensor_tensor(bvr[:, :], bvr[:, :], bv3[:, 1, :], ALU.subtract))
            prep(dve.tensor_copy(bv3[:, 2, :], bvr[:, :]))
            rows = bv_rows[:, :].rearrange("p (t f) -> p t f", f=D)
            part = [bv3[:, k, :].unsqueeze(1).broadcast_to([P, T, D]) for k in range(3)]
            prep(dve.tensor_scalar(rows, part[0], ident[:, 0:1], None, ALU.mult))
            for k in (1, 2):
                prep(dve.scalar_tensor_tensor(out=rows, in0=part[k], scalar=ident[:, k:k + 1], in1=rows,
                                              op0=ALU.mult, op1=ALU.add))
            prep(dve.memset(ones3[:, :], 1.0))
            prep(dve.memset(bkrep[:, :], 0.0))
            prep(dve.tensor_scalar(bkrep[:, :], bkrep[:, :], v1(BK1), None, ALU.add))

            causal_b = causal[:, :].unsqueeze(1).broadcast_to([P, T, D])
            pos_b = pos2[:, :].unsqueeze(1).broadcast_to([P, T, D])
            RSQRT = 11
            PRE_CHAIN = 5 + RSQRT

            def rsqrt_chain(step, v, y, t):
                step(dve.tensor_scalar(y.bitcast(I32), v.bitcast(I32), 1, None, ALU.logical_shift_right))
                step(dve.tensor_scalar(y.bitcast(I32), y.bitcast(I32), -1.0, RSQRT_MAGIC, ALU.mult, ALU.add))
                for _ in range(3):
                    step(dve.tensor_tensor(t, v, y, ALU.mult))
                    step(dve.scalar_tensor_tensor(out=t, in0=t, scalar=-0.5, in1=y, op0=ALU.mult, op1=ALU.mult))
                    step(dve.scalar_tensor_tensor(out=y, in0=t, scalar=1.5, in1=y, op0=ALU.add, op1=ALU.mult))

            def flat(k):
                return st[:, k, :, :].rearrange("p u t -> p (u t)")

            def pre_seq(i):
                for u in range(U):
                    n = i * U + u
                    m = mask[:, bass.ds(n * T, T)]
                    if not isinstance(i, int) or i > 0:
                        dve.wait_ge(p_seqT, (i - 1) * U + u + 1)
                    dve.wait_ge(s_gath[u], (i + 1) * (16 * T))
                    dve.tensor_tensor(tiles(seq, u), tiles(emb, u), pos_b, ALU.add).then_inc(s_raw, 1)
                    dve.wait_ge(s_raw, n + 1)
                    dve.tensor_tensor(tiles(seq, u), tiles(seq, u), spread(m), ALU.mult).then_inc(s_seq, 1)

            def pre_bn(i, u):
                dve.wait_ge(s_seq, i * U + u + 1)
                for t in range(T):
                    last = dve.bn_stats(stat[:, u, t, :], seq[:, u, D * t:D * t + D])
                last.then_inc(s_stat, 1)

            def pre_rstd(i):
                k = [0]

                def step(ins):
                    k[0] += 1
                    ins.then_inc(s_pre, 1)
                    dve.wait_ge(s_pre, i * PRE_CHAIN + k[0])

                dve.wait_ge(s_stat, i * U + U)
                me, Me = stat[:, :, :, 1], stat[:, :, :, 2]
                mo, Mo = stat[:, :, :, 4], stat[:, :, :, 5]
                step(dve.tensor_tensor(st[:, SUM, :, :], me, mo, ALU.add))
                step(dve.tensor_tensor(st[:, DIF, :, :], me, mo, ALU.subtract))
                step(dve.tensor_tensor(flat(DIF), flat(DIF), flat(DIF), ALU.mult))
                dve.tensor_tensor(st[:, TMP, :, :], Me, Mo, ALU.add).then_inc(s_m2, 1)
                dve.tensor_scalar(flat(MEAN), flat(SUM), 0.5, None, ALU.mult).then_inc(s_mean, 1)
                dve.wait_ge(s_m2, i + 1)
                step(dve.scalar_tensor_tensor(out=flat(TMP), in0=flat(DIF), scalar=D / 4.0, in1=flat(TMP),
                                              op0=ALU.mult, op1=ALU.add))
                step(dve.tensor_scalar(flat(VAR), flat(TMP), 1.0 / D, EPS, ALU.mult, ALU.add))
                rsqrt_chain(step, flat(VAR), flat(RSTD), flat(TMP))

            def pre_norm(i):
                dve.wait_ge(s_mean, i + 1)
                for u in range(U):
                    n = i * U + u
                    if not isinstance(i, int) or i > 0:
                        dve.wait_ge(p_xT, (i - 1) * U + u + 1)
                        dve.wait_ge(s_xg, (i - 1) * U + u + 1)
                    dve.tensor_tensor(tiles(xn, u), tiles(seq, u), spread(st[:, MEAN, u, :]),
                                      ALU.subtract).then_inc(s_shift, 1)
                    dve.wait_ge(s_shift, n + 1)
                    dve.tensor_tensor(tiles(xn, u), tiles(xn, u), spread(st[:, RSTD, u, :]),
                                      ALU.mult).then_inc(s_xn, 1)
                dve.tensor_scalar(koff[:, :], flat(SUM), 0.0, KEY_OFF, ALU.is_equal, ALU.mult).then_inc(s_koff, 1)

            def front_qmask(i):
                for u in range(U):
                    dve.wait_ge(s_xg, i * U + u + 1)
                    dve.tensor_reduce(st[:, XSUM, u, :], tiles(xg, u), AX.X, ALU.add).then_inc(s_xsum, 1)
                dve.wait_ge(s_xsum, i * U + U)
                nat = st[:, XSUM, :, :].rearrange("p u (j h) -> p (u j) h", h=2)
                scl = st[:, QMASK, :, :].rearrange("p u (j s) -> p (u j) s", s=2)
                for h in range(2):
                    for s in range(2):
                        last = dve.tensor_scalar(scl[D * h:D * h + D, :, s], nat[D * s:D * s + D, :, h],
                                                 wmean[D * s:D * s + D, 4:5], 0.0, ALU.add, ALU.not_equal)
                last.then_inc(s_qm, 1)

            def front_scores(i):
                for u in range(U):
                    n = i * U + u
                    dve.wait_ge(p_S, n + 1)
                    if not isinstance(i, int) or i > 0:
                        dve.wait_ge(p_PT, (i - 1) * U + u + 1)
                    sc = front[u][:, :].rearrange("p (t k) -> p t k", k=D)
                    dve.scalar_tensor_tensor(out=tiles(att, u), in0=sc, scalar=NEG, in1=causal_b,
                                             op0=ALU.max, op1=ALU.min).then_inc(s_S, 1)
                    dve.wait_ge(s_S, n + 1)
                    dve.tensor_reduce(st[:, NMAX, u, :], tiles(att, u), AX.X, ALU.max,
                                      negate=True).then_inc(s_max, 1)

            def front_norm(i, u):
                n = i * U + u
                dve.wait_ge(s_exp, n + 1)
                dve.reciprocal(st[:, INV, u, :], st[:, ESUM, u, :]).then_inc(s_rec, 1)
                dve.wait_ge(s_rec, n + 1)
                dve.wait_ge(s_qm, i + 1)
                dve.tensor_tensor(st[:, INV, u, :], st[:, INV, u, :], st[:, QMASK, u, :],
                                  ALU.mult).then_inc(s_inv, 1)
                dve.wait_ge(s_inv, n + 1)
                dve.tensor_tensor(tiles(att, u), tiles(att, u), spread(st[:, INV, u, :]),
                                  ALU.mult).then_inc(s_P, 1)

            def back_square_sum(i, u):
                dve.wait_ge(s_sq, i * U + u + 1)
                dve.tensor_reduce(st[:, SQ, u, :], tiles(zq, u), AX.X, ALU.add).then_inc(s_ss, 1)

            def back_norm(i):
                k = [0]

                def step(ins):
                    k[0] += 1
                    ins.then_inc(s_var2, 1)
                    dve.wait_ge(s_var2, i * (1 + RSQRT) + k[0])

                dve.wait_ge(s_ss, i * U + U)
                step(dve.tensor_scalar(flat(VAR2), flat(SQ), 1.0 / D, EPS, ALU.mult, ALU.add))
                rsqrt_chain(step, flat(VAR2), flat(RSTD2), flat(TMP2))
                for u in range(U):
                    z = back(0, u)[:, :].rearrange("p (t f) -> p t f", f=D)
                    dve.tensor_tensor(tiles(zn_, u), z, spread(st[:, RSTD2, u, :]), ALU.mult).then_inc(s_zn, 1)

            def back_out(i):
                for u in range(U):
                    n = i * U + u
                    if not isinstance(i, int) or i > 0:
                        dve.wait_ge(c_pS, i)
                    dve.wait_ge(p_Y, n + 1)
                    dve.scalar_tensor_tensor(out=seq2T[:, u, :], in0=back(3, u)[:, :], scalar=v1(B20),
                                             in1=x2T[:, u, :], op0=ALU.add, op1=ALU.add).then_inc(s_seq2T, 1)
                dve.wait_ge(s_seq2T, i * U + U)
                cols = seq2T[:, :, :].rearrange("p u (c q) -> p u c q", q=D)[:, :, :, D - 1]
                dve.tensor_tensor(xl[:, 0, :].rearrange("p (u c) -> p u c", u=U), cols,
                                  mlast[:, bass.ds(i * LC, LC)].rearrange("p (u c) -> p u c", u=U),
                                  ALU.mult).then_inc(c_last, 1)

            def back_tokens(i):
                for u in range(U):
                    n = i * U + u
                    if not isinstance(i, int) or i > 0:
                        dve.wait_ge(c_pO, i)
                    dve.wait_ge(p_seq2, n + 1)
                    m = mask[:, bass.ds(n * T, T)]
                    dve.tensor_tensor(tiles(seq2, u), back(4, u)[:, :].rearrange("p (t f) -> p t f", f=D),
                                      spread(m), ALU.mult).then_inc(s_seq2, 1)

            def back_key_mask(i):
                for u in range(U):
                    dve.wait_ge(s_seq2, i * U + u + 1)
                    last = dve.tensor_reduce(st[:, KSUM, u, :], tiles(seq2, u), AX.X, ALU.add)
                last.then_inc(s_ksum2, 1)
                dve.wait_ge(s_ksum2, i + 1)
                dve.tensor_scalar(koff2[:, :], flat(KSUM), 0.0, KEY_OFF,
                                  ALU.is_equal, ALU.mult).then_inc(s_koff2, 1)

            def last_centre(i):
                dve.wait_ge(c_pc, i + 1)
                dve.tensor_copy(xl[:, 1, :], spare[:, 0:LC]).then_inc(c_cen, 1)
                dve.wait_ge(c_cen, i + 1)
                dve.tensor_tensor(xl[:, 2, :], xl[:, 1, :], xl[:, 1, :], ALU.mult).then_inc(c_sq, 1)

            def last_norm(i):
                k = [0]

                def step(ins):
                    k[0] += 1
                    ins.then_inc(c_var, 1)
                    dve.wait_ge(c_var, i * (1 + RSQRT) + k[0])

                dve.wait_ge(c_pv, i + 1)
                step(dve.tensor_scalar(xl[:, 3, :], spare[:, 0:LC], EPS, None, ALU.add))
                rsqrt_chain(step, xl[:, 3, :], xl[:, 4, :], xl[:, 6, :])
                dve.tensor_tensor(xl[:, 5, :], xl[:, 1, :], xl[:, 4, :], ALU.mult).then_inc(c_xn, 1)

            def last_scores(i):
                dve.wait_ge(c_pS, i + 1)
                dve.scalar_tensor_tensor(out=s2[:, :], in0=spare[:, :], scalar=NEG, in1=diag2[:, :],
                                         op0=ALU.max, op1=ALU.min).then_inc(c_S, 1)
                dve.wait_ge(c_S, i + 1)
                dve.tensor_reduce(s2v[:, 0:1], s2[:, :], AX.X, ALU.max, negate=True).then_inc(c_max, 1)

            def last_probs(i):
                dve.wait_ge(c_exp, i + 1)
                dve.reciprocal(s2v[:, 2:3], s2v[:, 1:2]).then_inc(c_inv, 1)
                dve.wait_ge(c_inv, i + 1)
                dve.tensor_scalar(s2[:, :], s2[:, :], s2v[:, 2:3], None, ALU.mult).then_inc(c_P, 1)

            def last_attended(i):
                dve.wait_ge(c_pO, i + 1)
                dve.tensor_copy(o2[:, :], spare[:, 0:P]).then_inc(c_O, 1)

            def last_store(i):
                dve.wait_ge(c_pOT, i + 1)
                src = spare[:, 0:P].rearrange("p (u m) -> p u m", u=U)
                for h in range(2):
                    a, b = D * h, D * h + D
                    last = dve.tensor_copy(OT[a:b, bass.ds(i * LC, LC)].rearrange("p (u c) -> p u c", u=U),
                                           src[a:b, :, 2 * J * h:2 * J * h + 2 * J])
                last.then_inc(c_OT, 1)

            def body(i, p, a, b, c):
                if p:
                    pre_seq(i + 1)
                for u in range(U):
                    if b:
                        back_square_sum(i - 1, u)
                    if p and u > 1:
                        pre_bn(i + 1, u - 2)
                if b:
                    back_norm(i - 1)
                if p:
                    pre_bn(i + 1, 2)
                    pre_bn(i + 1, 3)
                    pre_rstd(i + 1)
                if c:
                    last_scores(i - 2)
                if p:
                    pre_norm(i + 1)
                if c:
                    last_probs(i - 2)
                if a:
                    front_qmask(i)
                    front_scores(i)
                if c:
                    last_attended(i - 2)
                if b:
                    back_out(i - 1)
                if c:
                    last_store(i - 2)
                if a:
                    front_norm(i, 0)
                if b:
                    back_tokens(i - 1)
                if a:
                    front_norm(i, 1)
                if b:
                    last_centre(i - 1)
                if a:
                    front_norm(i, 2)
                    front_norm(i, 3)
                if b:
                    back_key_mask(i - 1)
                    last_norm(i - 1)

            pre_seq(0)
            for u in range(U):
                pre_bn(0, u)
            pre_rstd(0)
            pre_norm(0)
            body(0, True, True, False, False)
            body(1, True, True, True, False)
            with dve.Fori(2, STEPS - 1) as i:
                body(i, True, True, True, True)
            body(STEPS - 1, False, True, True, True)
            body(STEPS, False, False, True, True)

            def split(c, slot):
                dve.wait_ge(i_hi, c + 1)
                if not isinstance(c, int) or c > 0:
                    dve.wait_ge(i_xy, c)
                dve.tensor_tensor(irem, it32[0 if slot % 2 == 0 else 1], ix[slot][0:D, :],
                                  ALU.subtract).then_inc(i_rem, 1)
                dve.wait_ge(i_rem, c + 1)
                dve.tensor_copy(imid[:, :], irem).then_inc(i_mid, 1)
                dve.wait_ge(i_mid, c + 1)
                dve.tensor_copy(ix[slot][D:P, :], imid[:, :])
                dve.tensor_tensor(iy[slot][0:D, :], irem, imid[:, :], ALU.subtract).then_inc(i_xy, 1)

            def drain_even(c, k, free=None):
                if free is not None:
                    dve.wait_ge(o_st[k], free)
                for t in range(NT):
                    dve.wait_ge(i_mm, c * NT * 2 + 2 * t + 1)
                    dve.tensor_copy(ost[k * NT + t][:, 0:NB], banks[2 * t][:, 0:NB]).then_inc(o_even, 1)

            split(0, 0)
            split(1, 1)
            body(STEPS + 1, False, False, False, True)

            def own(ins, k=[0]):
                k[0] += 1
                ins.then_inc(e_dve, 1)
                dve.wait_ge(e_dve, k[0])

            def rsqrt():
                own(dve.reciprocal(zr, zr))
                own(dve.tensor_tensor(zt, zv, zr, ALU.mult))
                own(dve.tensor_tensor(zt, zt, zr, ALU.mult))
                own(dve.tensor_scalar(zt, zt, -0.5, 1.5, ALU.mult, ALU.add))
                own(dve.tensor_tensor(zr, zr, zt, ALU.mult))

            dve.wait_ge(c_OT, STEPS)
            dve.drain().then_inc(e_go, 1)
            dve.wait_ge(e_pe, 2)
            own(dve.tensor_scalar(qml, hi[1][:, 0:QL], 0.0, None, ALU.not_equal))
            own(dve.scalar_tensor_tensor(out=za, in0=hi[0][:, 0:QL], scalar=v1(BV1), in1=qml,
                                         op0=ALU.add, op1=ALU.mult))
            own(dve.tensor_tensor(za, za, XL[:, :], ALU.add))
            dve.wait_ge(e_pe, 3)
            own(dve.tensor_copy(zc, lo[0][:, 0:QL]))
            dve.wait_ge(e_pe, 4)
            dve.tensor_scalar(zv, lo[1][:, 0:QL], EPS, None, ALU.add).then_inc(e_var, 1)
            dve.wait_ge(e_act, 2)
            rsqrt()
            own(dve.tensor_tensor(zn, zc, zr, ALU.mult))
            dve.wait_ge(e_act, 3)
            dve.wait_ge(e_pe, 6)
            own(dve.scalar_tensor_tensor(out=zy, in0=lo[3][:, 0:QL], scalar=v1(B21), in1=zx,
                                         op0=ALU.add, op1=ALU.add))
            own(dve.tensor_tensor(zy, zy, mlast[:, :], ALU.mult))
            dve.wait_ge(e_pe, 7)
            own(dve.tensor_copy(zc, hi[2][:, 0:QL]))
            dve.wait_ge(e_pe, 8)
            dve.tensor_scalar(zv, hi[3][:, 0:QL], EPS, None, ALU.add).then_inc(e_var, 1)
            dve.wait_ge(e_act, 6)
            rsqrt()
            own(dve.tensor_tensor(zn, zc, zr, ALU.mult))
            dve.wait_ge(e_act, 7)
            ftv = FT.rearrange("p (g h s) -> p g h s", h=2, s=2)
            zxv = zx.rearrange("p (g s) -> p g s", s=2)
            for dup in range(2):
                for h in range(2):
                    own(dve.tensor_copy(ftv[D * dup:D * dup + D, :, h, :], zxv[D * h:D * h + D, :, :]))
            own(dve.tensor_copy(f_hi[:, :], FT))
            own(dve.tensor_tensor(FR, FT, f_hi[:, :], ALU.subtract))
            own(dve.tensor_copy(f_mid[:, :], FR))
            own(dve.tensor_copy(f_hl[0:D, :], f_hi[0:D, :]))
            dve.tensor_tensor(f_hl[D:P, :], FR[D:P, :], f_mid[D:P, :], ALU.subtract).then_inc(f_split, 1)

            split(2, 2)
            for c in range(FIRST):
                split(c + AHEAD, (c + AHEAD) % SLOTS)
                drain_even(c, c)
            with dve.Fori(0, ROUNDS) as rd:
                for q in range(SLOTS):
                    c = rd * SLOTS + (FIRST + q)
                    split(c + AHEAD, (FIRST + q + AHEAD) % SLOTS)
                    drain_even(c, q % 2, (rd * (SLOTS // 2) + (FIRST + q) // 2) * (16 * NT))
            for c in range(CH - AHEAD, CH):
                drain_even(c, c % 2, (c // 2) * (16 * NT))

        @block.scalar
        def _(act):
            def front_copy(i, out, p_sem, s_sem, func=ACT.Copy, **kw):
                for u in range(U):
                    act.wait_ge(p_sem, i * U + u + 1)
                    act.activation(out[:, u, :], front[u][:, :], func, **kw).then_inc(s_sem, 1)

            def front_values(i):
                for u in range(U):
                    if not isinstance(i, int) or i > 0:
                        act.wait_ge(p_z, (i - 1) * U + u + 1)
                    act.wait_ge(p_V, i * U + u + 1)
                    act.activation(V[:, u, :], front[u][:, :], ACT.Copy).then_inc(s_V, 1)

            def front_koffT(i):
                act.wait_ge(p_koff, i + 1)
                act.activation(koffT[:, :], front[0][0:U * T, 0:P], ACT.Copy).then_inc(s_koffT, 1)

            def front_exp(i):
                for u in range(U):
                    act.wait_ge(s_max, i * U + u + 1)
                    for t in range(T):
                        blk = att[:, u, D * t:D * t + D]
                        last = act.activation(blk, blk, ACT.Exp, bias=st[:, NMAX, u, t:t + 1],
                                              accum_out=st[:, ESUM, u, t:t + 1])
                    last.then_inc(s_exp, 1)

            def back_copy(i, k, out, p_sem, s_sem, func, groups=range(U), **kw):
                for u in groups:
                    act.wait_ge(p_sem, i * U + u + 1)
                    act.activation(out[:, u, :], back(k, u)[:, :], func, **kw).then_inc(s_sem, 1)

            def last_keys(i):
                act.wait_ge(c_pk, i + 1)
                act.activation(koffT2[:, :], spare[0:U * T, 0:P], ACT.Copy).then_inc(c_kT, 1)

            def last_affine(i):
                act.wait_ge(c_xn, i + 1)
                act.activation(xl[:, 7, :], xl[:, 5, :], ACT.Identity, bias=v1(LN1B1),
                               scale=v1(LN1G1)).then_inc(c_x, 1)
                act.activation(XL[:, bass.ds(i * LC, LC)], xl[:, 5, :], ACT.Identity, bias=v1(LN1B1),
                               scale=v1(LN1G1)).then_inc(c_XL, 1)

            def last_query(i):
                act.wait_ge(c_pq, i + 1)
                for h in range(2):
                    a, b = D * h, D * h + D
                    last = act.activation(QB[a:b, :, 2 * J * h:2 * J * h + 2 * J],
                                          spare[a:b, 0:LC].rearrange("p (u c) -> p u c", u=U), ACT.Identity,
                                          bias=vec8[a:b, 1:2], scale=0.125)
                last.then_inc(c_QB, 1)

            def last_weighted(i):
                act.wait_ge(c_pa, i + 1)
                act.activation(AB[:, :, :].rearrange("p u c -> p (u c)"), spare[:, 0:P],
                               ACT.Copy).then_inc(c_AB, 1)

            def last_exp(i):
                act.wait_ge(c_max, i + 1)
                act.activation(s2[:, :], s2[:, :], ACT.Exp, bias=s2v[:, 0:1],
                               accum_out=s2v[:, 1:2]).then_inc(c_exp, 1)

            def last_turned(i):
                act.wait_ge(c_pPT, i + 1)
                act.activation(PT2[:, :], spare[:, :], ACT.Copy).then_inc(c_PT, 1)

            def body(i, a, b, c):
                if a:
                    front_copy(i, seqT, p_seqT, s_seqT)
                if c:
                    last_affine(i - 2)
                if b:
                    back_copy(i - 1, 0, zq, p_z, s_sq, ACT.Square, (0,))
                if c:
                    last_query(i - 2)
                if b:
                    back_copy(i - 1, 0, zq, p_z, s_sq, ACT.Square, (1, 2))
                if c:
                    last_weighted(i - 2)
                if b:
                    back_copy(i - 1, 0, zq, p_z, s_sq, ACT.Square, (3,))
                if a:
                    front_copy(i, KT, p_K, s_K, ACT.Identity, bias=v1(BK0))
                    front_values(i)
                if c:
                    last_keys(i - 2)
                if a:
                    front_koffT(i)
                if b:
                    back_copy(i - 1, 1, x2T, p_x2T, s_x2T, ACT.Identity, bias=v1(LN2B0), scale=v1(LN2G0))
                if a:
                    front_copy(i, xT, p_xT, s_xT, ACT.Identity, bias=v1(LN1B0), scale=v1(LN1G0))
                if c:
                    last_exp(i - 2)
                if b:
                    back_copy(i - 1, 2, HT, p_H, s_H, ACT.Relu, bias=v1(B10))
                if a:
                    front_copy(i, QT, p_Q, s_Q, ACT.Identity, bias=vec8[:, 0:1], scale=0.125)
                if c:
                    last_turned(i - 2)
                if a:
                    front_exp(i)
                    front_copy(i, PT, p_PT, s_PT)

            body(0, True, False, False)
            body(1, True, True, False)
            with act.Fori(2, STEPS) as i:
                body(i, True, True, True)
            body(STEPS, False, True, True)

            def high(c, slot, loads):
                act.wait_ge(i_load[slot % 2], loads * 16)
                if not isinstance(c, int) or c >= SLOTS:
                    act.wait_ge(i_mm, (c - (SLOTS - 1)) * (2 * NT))
                act.activation(ix[slot][0:D, :], it32[slot % 2], ACT.Copy).then_inc(i_hi, 1)
                act.wait_ge(i_hi, c + 1)
                act.activation(iy[slot][D:P, :], ix[slot][0:D, :], ACT.Copy).then_inc(i_hs, 1)

            def drain_odd(c, k, free=None):
                if free is not None:
                    act.wait_ge(o_st[k], free)
                for t in range(NT):
                    act.wait_ge(i_mm, c * NT * 2 + 2 * t + 2)
                    act.activation(ost[k * NT + t][:, NB:NC], banks[2 * t + 1][:, 0:NB],
                                   ACT.Copy).then_inc(o_odd, 1)

            high(0, 0, 1)
            high(1, 1, 1)
            body(STEPS + 1, False, False, True)

            act.wait_ge(e_dve, 4)
            act.activation(zs, lo[0][:, 0:QL], ACT.Square).then_inc(e_act, 1)
            act.wait_ge(e_var, 1)
            act.activation(zr, zv, ACT.Sqrt).then_inc(e_act, 1)
            act.wait_ge(e_dve, 10)
            act.activation(zx, zn, ACT.Identity, bias=v1(LN2B1), scale=v1(LN2G1)).then_inc(e_act, 1)
            act.wait_ge(e_pe, 5)
            act.activation(zh, lo[2][:, 0:QL], ACT.Relu, bias=v1(B11)).then_inc(e_act, 1)
            act.wait_ge(e_dve, 13)
            act.activation(zs, hi[2][:, 0:QL], ACT.Square).then_inc(e_act, 1)
            act.wait_ge(e_var, 2)
            act.activation(zr, zv, ACT.Sqrt).then_inc(e_act, 1)
            act.wait_ge(e_dve, 19)
            act.activation(zx, zn, ACT.Identity, bias=v1(LNFB), scale=v1(LNFG)).then_inc(e_act, 1)

            for c in range(2, FIRST + AHEAD):
                high(c, c % SLOTS, c // 2 + 1)
                if c >= AHEAD:
                    drain_odd(c - AHEAD, c - AHEAD)
            with act.Fori(0, ROUNDS) as rd:
                for q in range(SLOTS):
                    c = rd * SLOTS + (FIRST + q)
                    high(c + AHEAD, (FIRST + q + AHEAD) % SLOTS, rd * (SLOTS // 2) + ((FIRST + q + AHEAD) // 2 + 1))
                    drain_odd(c, q % 2, (rd * (SLOTS // 2) + (FIRST + q) // 2) * (16 * NT))
            for c in range(CH - AHEAD, CH):
                drain_odd(c, c % 2, (c // 2) * (16 * NT))

        @block.tensor
        def _(pe):
            def mm(o, l, r, start=True):
                return pe.matmul(o, l, r, start=start, stop=True, skip_group_check=True)

            def turn(bank, src):
                for j in range(J):
                    last = pe.transpose(bank[:, P * j:P * j + P], src[:, P * j:P * j + P], ident[:, :])
                return last

            pe.wait_ge(s_prep, n_prep[0])
            pe.wait_ge(s_const, n_const[0])

            def front_seqT(i):
                for u in range(U):
                    n = i * U + u
                    if not isinstance(i, int) or i > 0:
                        pe.wait_ge(s_PT, (i - 1) * U + u + 1)
                    pe.wait_ge(s_seq, n + 1)
                    turn(front[u], seq[:, u, :]).then_inc(p_seqT, 1)

            def front_keys(i):
                for u in range(U):
                    pe.wait_ge(s_seqT, i * U + u + 1)
                    mm(front[u][:, :], wbd[:, WK0, :], seqT[:, u, :]).then_inc(p_K, 1)

            def front_values(i):
                for u in range(U):
                    pe.wait_ge(s_K, i * U + u + 1)
                    mm(front[u][:, :], ones3[:, :], bv_rows[0:3, :])
                    for j in range(J):
                        last = mm(front[u][:, P * j:P * j + P], seqT[:, u, P * j:P * j + P], wbd[:, WV0, :], False)
                    last.then_inc(p_V, 1)

            def front_koffT(i):
                pe.wait_ge(s_V, i * U + 1)
                pe.wait_ge(s_koff, i + 1)
                pe.transpose(front[0][0:U * T, 0:P], koff[:, :], ident[:, :]).then_inc(p_koff, 1)

            def front_xT(i):
                pe.wait_ge(s_koffT, i + 1)
                for u in range(U):
                    n = i * U + u
                    pe.wait_ge(s_V, n + 1)
                    pe.wait_ge(s_xn, n + 1)
                    turn(front[u], xn[:, u, :]).then_inc(p_xT, 1)

            def front_query(i):
                for u in range(U):
                    pe.wait_ge(s_xT, i * U + u + 1)
                    mm(front[u][:, :], wbd[:, WQ0, :], xT[:, u, :]).then_inc(p_Q, 1)

            def front_scores(i):
                for u in range(U):
                    pe.wait_ge(s_Q, i * U + u + 1)
                    for j in range(J):
                        mm(front[u][:, P * j:P * j + P], sel1[:, (u * J + j) * P:(u * J + j) * P + P],
                           koffT[:, :], j == 0)
                    for h in range(2):
                        a, b = D * h, D * h + D
                        for c in range(T):
                            last = mm(front[u][a:b, D * c:D * c + D], QT[a:b, u, D * c:D * c + D],
                                      KT[a:b, u, D * c:D * c + D], False)
                    last.then_inc(p_S, 1)

            def front_turn(i, groups):
                for u in groups:
                    pe.wait_ge(s_P, i * U + u + 1)
                    turn(front[u], att[:, u, :]).then_inc(p_PT, 1)

            def back_room(i, u, before, same):
                if u < U - 1:
                    pe.wait_ge(before, i * U + u + 2)
                else:
                    pe.wait_ge(same, i * U + 1)

            def back_hidden(i):
                for u in range(U):
                    back_room(i, u, s_x2T, s_H)
                    pe.wait_ge(s_x2T, i * U + u + 1)
                    mm(back(2, u)[:, :], wbd[:, W10, :], x2T[:, u, :]).then_inc(p_H, 1)

            def back_out(i):
                for u in range(U):
                    back_room(i, u, s_H, s_seq2T)
                    pe.wait_ge(s_H, i * U + u + 1)
                    mm(back(3, u)[:, :], wbd[:, W20, :], HT[:, u, :]).then_inc(p_Y, 1)

            def last_weighted(i):
                pe.wait_ge(c_QB, i + 1)
                mm(spare[:, 0:P], wbd[:, WKT1, :], QB[:, :, :].rearrange("p u c -> p (u c)")).then_inc(c_pa, 1)

            def last_scores(i):
                pe.wait_ge(c_kT, i + 1)
                for j in range(J):
                    mm(spare[:, P * j:P * j + P], sel2[:, P * j:P * j + P], koffT2[:, :], j == 0)
                mm(spare[:, :], QB[:, :, :].rearrange("p u c -> p (u c)"), bkrep[:, :], False)
                for u in range(U):
                    last = mm(spare[ROWS * u:ROWS * u + ROWS, :], AB[:, u, :], seq2T[:, u, :], False)
                last.then_inc(c_pS, 1)

            def last_turn(i):
                pe.wait_ge(c_P, i + 1)
                turn(spare, s2[:, :]).then_inc(c_pPT, 1)

            def last_attend(i):
                pe.wait_ge(c_PT, i + 1)
                for u in range(U):
                    for j in range(J):
                        last = mm(spare[ROWS * u:ROWS * u + ROWS, 0:P],
                                  PT2[:, P * j + ROWS * u:P * j + ROWS * u + ROWS],
                                  seq2[:, u, P * j:P * j + P], j == 0)
                last.then_inc(c_pO, 1)

            def last_back(i):
                pe.wait_ge(c_O, i + 1)
                pe.transpose(spare[:, 0:P], o2[:, :], ident[:, :]).then_inc(c_pOT, 1)

            def back_z(i, groups):
                for u in groups:
                    if not isinstance(i, int) or i > 0:
                        if u < U - 1:
                            pe.wait_ge(s_seq2, i * U)
                        else:
                            pe.wait_ge(c_AB, i)
                    pe.wait_ge(s_PT, i * U + u + 1)
                    for j in range(J):
                        mm(back(0, u)[:, P * j:P * j + P], xT[:, u, P * j:P * j + P], center[:, :], j == 0)
                    for s in range(2):
                        a, b = D * s, D * s + D
                        for t in range(T):
                            last = mm(back(0, u)[a:b, D * t:D * t + D], PT[a:b, u, D * t:D * t + D],
                                      V[a:b, u, D * t:D * t + D], False)
                    last.then_inc(p_z, 1)

            def back_x2T(i):
                for u in range(U):
                    if u == U - 1:
                        pe.wait_ge(s_x2T, i * U + 1)
                    pe.wait_ge(s_zn, i * U + u + 1)
                    turn(back(1, u), zn_[:, u, :]).then_inc(p_x2T, 1)

            def back_tokens(i):
                for u in range(U):
                    back_room(i, u, s_seq2T, s_seq2)
                    pe.wait_ge(s_seq2T, i * U + u + 1)
                    turn(back(4, u), seq2T[:, u, :]).then_inc(p_seq2, 1)

            def last_centre(i):
                if not isinstance(i, int) or i > 0:
                    pe.wait_ge(c_OT, i)
                pe.wait_ge(c_last, i + 1)
                mm(spare[:, 0:LC], center[:, :], xl[:, 0, :]).then_inc(c_pc, 1)

            def last_var(i):
                pe.wait_ge(c_sq, i + 1)
                mm(spare[:, 0:LC], mean_m[:, :], xl[:, 2, :]).then_inc(c_pv, 1)

            def last_query(i):
                pe.wait_ge(c_x, i + 1)
                mm(spare[:, 0:LC], wbd[:, WQ1, :], xl[:, 7, :]).then_inc(c_pq, 1)

            def last_keys(i, b):
                if b:
                    pe.wait_ge(s_zn, (i + 2) * U)
                else:
                    pe.wait_ge(c_AB, i + 1)
                pe.wait_ge(s_koff2, i + 1)
                pe.transpose(spare[0:U * T, 0:P], koff2[:, :], ident[:, :]).then_inc(c_pk, 1)

            def body(i, a, b, c):
                if a:
                    front_seqT(i)
                if b:
                    back_z(i - 1, (0,))
                if c:
                    last_query(i - 2)
                if b:
                    back_z(i - 1, (1, 2))
                if c:
                    last_weighted(i - 2)
                if b:
                    back_z(i - 1, (3,))
                if a:
                    front_keys(i)
                    front_values(i)
                if c:
                    last_keys(i - 2, b)
                if a:
                    front_koffT(i)
                if b:
                    back_x2T(i - 1)
                if c:
                    last_scores(i - 2)
                if a:
                    front_xT(i)
                if b:
                    back_hidden(i - 1)
                if a:
                    front_query(i)
                if c:
                    last_turn(i - 2)
                if a:
                    front_scores(i)
                if c:
                    last_attend(i - 2)
                if b:
                    back_out(i - 1)
                if c:
                    last_back(i - 2)
                if b:
                    back_tokens(i - 1)
                if a:
                    front_turn(i, (0, 1))
                if b:
                    last_centre(i - 1)
                if a:
                    front_turn(i, (2, 3))
                if b:
                    last_var(i - 1)

            body(0, True, False, False)
            body(1, True, True, False)
            with pe.Fori(2, STEPS) as i:
                body(i, True, True, True)
            body(STEPS, False, True, True)
            body(STEPS + 1, False, False, True)

            pe.wait_ge(c_OT, STEPS)
            mm(hi[0][:, 0:QL], wbd[:, WV1, :], OT[:, :]).then_inc(e_pe, 1)
            mm(hi[1][:, 0:QL], mean_m[:, :], XL[:, :]).then_inc(e_pe, 1)
            pe.wait_ge(e_dve, 3)
            mm(lo[0][:, 0:QL], center[:, :], za).then_inc(e_pe, 1)
            pe.wait_ge(e_act, 1)
            mm(lo[1][:, 0:QL], mean_m[:, :], zs).then_inc(e_pe, 1)
            pe.wait_ge(e_act, 3)
            mm(lo[2][:, 0:QL], wbd[:, W11, :], zx).then_inc(e_pe, 1)
            pe.wait_ge(e_act, 4)
            mm(lo[3][:, 0:QL], wbd[:, W21, :], zh).then_inc(e_pe, 1)
            pe.wait_ge(e_dve, 12)
            mm(hi[2][:, 0:QL], center[:, :], zy).then_inc(e_pe, 1)
            pe.wait_ge(e_act, 5)
            mm(hi[3][:, 0:QL], mean_m[:, :], zs).then_inc(e_pe, 1)

            pe.wait_ge(f_split, 1)

            def product(c, slot):
                pe.wait_ge(i_xy, c + 1)
                pe.wait_ge(i_hs, c + 1)
                for t in range(NT):
                    for half in range(2):
                        b = banks[2 * t + half]
                        if not isinstance(c, int) or c > 0:
                            pe.wait_ge(o_even if half == 0 else o_odd, (c - 1) * NT + t + 1)
                        xs = ix[slot][:, NB * half:NB * half + NB]
                        ys = iy[slot][:, NB * half:NB * half + NB]
                        mm(b[:, 0:NB], f_hi[:, P * t:P * t + P], xs)
                        mm(b[:, 0:NB], f_mid[:, P * t:P * t + P], xs, False)
                        last = mm(b[:, 0:NB], f_hl[:, P * t:P * t + P], ys, False)
                        last.then_inc(i_mm, 1)

            product(0, 0)
            with pe.Fori(0, CH // SLOTS) as rd:
                for q in range(SLOTS):
                    product(rd * SLOTS + (1 + q), (1 + q) % SLOTS)


def kernel(r_input_ids, L0_rec_item_emb, L0_rec_pos_emb, L0_rec_ln1_g, L0_rec_ln1_b, L0_rec_Wq, L0_rec_bq,
           L0_rec_Wk, L0_rec_bk, L0_rec_Wv, L0_rec_bv, L0_rec_ln2_g, L0_rec_ln2_b, L0_rec_W1, L0_rec_b1,
           L0_rec_W2, L0_rec_b2, L0_rec_lnf_g, L0_rec_lnf_b, L0_rec_out_item_emb):
    import numpy as np
    import concourse.bacc as bacc
    from concourse.bass_utils import run_bass_kernel_spmd

    a = lambda x: np.ascontiguousarray(x)
    ids = np.asarray(r_input_ids)
    nb = ids.shape[0]
    groups = nb // (2 * T)
    g1, b1_, bq, bk, bv = (np.asarray(x) for x in (L0_rec_ln1_g, L0_rec_ln1_b, L0_rec_bq, L0_rec_bk, L0_rec_bv))
    g2, b2_, f1, f2 = (np.asarray(x) for x in (L0_rec_ln2_g, L0_rec_ln2_b, L0_rec_b1, L0_rec_b2))
    wq, wk, wv, w1, w2 = (np.asarray(x) for x in (L0_rec_Wq, L0_rec_Wk, L0_rec_Wv, L0_rec_W1, L0_rec_W2))
    vec_list = [g1[0], b1_[0], bq[0], bk[0], g2[0], b2_[0], f1[0], f2[0],
                g1[1], b1_[1], bq[1], bv[1], g2[1], b2_[1], f1[1], f2[1],
                np.asarray(L0_rec_lnf_g), np.asarray(L0_rec_lnf_b), bk[1]]
    w_list = [wq[0], wk[0], wv[0], w1[0], w2[0], wq[1], wk[1].T, wv[1], w1[1], w2[1]]

    f = np.float32
    eye = np.eye(P, dtype=f)
    blocks = np.kron(np.eye(2, dtype=f), np.ones((D, D), f))
    q = np.arange(P) % D
    causal = np.where(np.arange(D)[None, :] <= q[:, None], f(3e38), f(NEG)).astype(f)
    sel1 = np.zeros((U, T, U, J, 2, D), f)
    sel2 = np.zeros((U, T, J, U, ROWS), f)
    diag2 = np.full((U, ROWS, J, 2, D), f(3e38), f)
    for u in range(U):
        for j in range(J):
            for h in range(2):
                sel1[u, 2 * j + h, u, j, h, :] = 1
                for jj in range(J):
                    for s in range(2):
                        m = (h * J + jj) * 2 + s
                        sel2[u, 2 * j + h, j, u, m] = 1
                        if (jj, s) != (j, 0):
                            diag2[u, m, j, 0, :] = -1e38
                        if (jj, s) != (j, 1):
                            diag2[u, m, j, 1, :] = -1e38
    arrays = {
        "ids_tok": a(ids.reshape(-1, P).T),
        "ids_last": a(ids[:, -1].reshape(groups, J, 2, 2).transpose(2, 0, 1, 3).reshape(2, -1)),
        "item_emb": a(L0_rec_item_emb),
        "vecs": a(np.stack(vec_list, 1)),
        "weights": a(np.stack(w_list, 1)),
        "pos": a(L0_rec_pos_emb),
        "bv_row": a(bv[0:1]),
        "ln_rows": a(np.stack([g1[0], b1_[0]])),
        "items_t": a(np.asarray(L0_rec_out_item_emb).T),
        "ident_c": eye,
        "center_c": (eye - blocks / D).astype(f),
        "mean_c": (blocks / D).astype(f),
        "causal_c": causal,
        "diag2_c": diag2.reshape(P, W),
        "sel1_c": sel1.reshape(U * T, -1),
        "sel2_c": sel2.reshape(U * T, -1),
    }
    nc = bacc.Bacc("TRN2", target_bir_lowering=False, num_devices=1)
    args = [nc.dram_tensor(k, v.shape, mybir.dt.from_np(v.dtype), kind="ExternalInput").ap()
            for k, v in arrays.items()]
    out = nc.dram_tensor("scores_out", (nb, L0_rec_out_item_emb.shape[0]), F32, kind="ExternalOutput").ap()
    build(nc, *args, out)
    r = run_bass_kernel_spmd(nc, [arrays], core_ids=[0])
    return r.results[0]["scores_out"]
```

```python
from contextlib import ExitStack

import concourse.bass as bass
from concourse import mybir

F32 = mybir.dt.float32
BF16 = mybir.dt.bfloat16
I32 = mybir.dt.int32
ALU = mybir.AluOpType
ACT = mybir.ActivationFunctionType
AX = mybir.AxisListType

P = 128
D = 64
EPS = 0.001
NEG = -2.0 ** 32
KEY_OFF = -2.0 ** 100
U = 4
J = 4
W = J * P
T = 2 * J
RSQRT_MAGIC = float(0x5F3759DF)
(VAR, VAR2, VARL, RSTD, RSTD2, RSTDL, TMP, TMP2, TMPL,
 SUM, DIF, MEAN, NMAX, ESUM, INV, XSUM, QMASK, SQ, KSUM, NST) = range(20)
ROWS = 32

(LN1G0, LN1B0, BQ0, BK0, LN2G0, LN2B0, B10, B20,
 LN1G1, LN1B1, BQ1, BV1, LN2G1, LN2B1, B11, B21, LNFG, LNFB, BK1, NVEC) = range(20)
WQ0, WK0, WV0, W10, W20, WQ1, WKT1, WV1, W11, W21, NW = range(11)


def build(nc, ids_tok, ids_last, item_emb, vecs, weights, pos, bv_row, ln_rows, items_t,
          ident_c, center_c, mean_c, causal_c, diag2_c, sel1_c, sel2_c, out):
    n_tiles = ids_tok.shape[1]
    STEPS = n_tiles // (U * T)
    NITEMS = items_t.shape[1]
    B = out.shape[0]
    NROW = item_emb.shape[0]
    QL = B // 2
    LC = U * J * 2

    with ExitStack() as ctx:
        def sb(name, shape, dt=F32):
            return ctx.enter_context(nc.sbuf_tensor(name, shape, dt))

        def sem(name):
            return ctx.enter_context(nc.semaphore(name))

        banks = [ctx.enter_context(nc.psum_tensor(f"bank{i}", [P, 512], F32)) for i in range(8)]
        lo, hi = banks[:4], banks[4:]
        front = banks[:4]
        spare = banks[7]

        def back(stage, u):
            if stage == 0:
                return banks[4 + u]
            return banks[4 + ((stage - 1) * U + u) % 3]

        ident = sb("ident", [P, P])
        center = sb("center", [P, P])
        mean_m = sb("mean_m", [P, P])
        causal = sb("causal", [P, D])
        diag2 = sb("diag2", [P, W])
        sel1 = sb("sel1", [U * T, U * J * P], BF16)
        sel2 = sb("sel2", [U * T, J * P], BF16)
        vec = sb("vec", [P, NVEC])
        vec8 = sb("vec8", [P, 2])
        wbd = sb("wbd", [P, NW, P])
        wmean = sb("wmean", [P, 5])
        pos2 = sb("pos2", [P, D])
        bvr = sb("bvr", [P, D])
        gain_row = sb("gain_row", [P, D])
        bias_row = sb("bias_row", [P, D])
        bv3 = sb("bv3", [P, 3, D], BF16)
        bv_rows = sb("bv_rows", [P, W], BF16)
        ones3 = sb("ones3", [3, P], BF16)
        bkrep = sb("bkrep", [P, W])
        ids_i = sb("ids_i", [P, n_tiles], I32)
        ids_f = sb("ids_f", [P, n_tiles])
        ids_n = sb("ids_n", [P, n_tiles])
        idx = sb("idx", [P, n_tiles], I32)
        idx_now = sb("idx_now", [P, U * T], I32)
        mask = sb("mask", [P, n_tiles])
        idl_i = sb("idl_i", [P, QL], I32)
        mlast = sb("mlast", [P, QL])

        emb = sb("emb", [P, U, W])
        placed_emb = sb("placed_emb", [P, U, W])
        seq = sb("seq", [P, U, W])
        seqT = sb("seqT", [P, U, W])
        KT = sb("KT", [P, U, W])
        V = sb("V", [P, U, W])
        xn = sb("xn", [P, U, W])
        xT = sb("xT", [P, U, W])
        QT = sb("QT", [P, U, W])
        att = sb("att", [P, U, W])
        PT = sb("PT", [P, U, W])
        zq = sb("zq", [P, U, W])
        xg = sb("xg", [P, U, W])
        sel1f = zq[0:U * T, :, :].rearrange("p u w -> p (u w)")
        sel2f = xg[0:U * T, 0, :]
        x2T = sb("x2T", [P, U, W])
        HT = sb("HT", [P, U, W])
        seq2T = sb("seq2T", [P, U, W])
        seq2 = sb("seq2", [P, U, W])
        stat = sb("stat", [P, U, T, 6])
        st = sb("st", [P, NST, U, T])
        koff = sb("koff", [P, U * T])
        koffT = sb("koffT", [U * T, P], BF16)
        koff2 = sb("koff2", [P, U * T])
        koffT2 = sb("koffT2", [U * T, P], BF16)

        xl = sb("xl", [P, 8, LC])
        QB = sb("QB", [P, U, ROWS])
        AB = sb("AB", [P, U, ROWS])
        s2 = sb("s2", [P, W])
        s2v = sb("s2v", [P, 4])
        PT2 = sb("PT2", [P, W])
        o2 = sb("o2", [P, P])
        XL = sb("XL", [P, QL])
        OT = sb("OT", [P, QL])

        s_const = sem("s_const")
        s_ids = sem("s_ids")
        s_zero = sem("s_zero")
        s_prep = sem("s_prep")
        s_idx = sem("s_idx")
        s_now = sem("s_now")
        s_gath = [sem(f"s_gath{u}") for u in range(U)]
        s_room = sem("s_room")
        s_raw = sem("s_raw")
        s_raw_dve = sem("s_raw_dve")
        s_xg_dve = sem("s_xg_dve")
        s_seq = sem("s_seq")
        s_stat = sem("s_stat")
        s_rsq = sem("s_rsq")
        s_var = sem("s_var")
        s_dif = sem("s_dif")
        s_sum = sem("s_sum")
        s_m2 = sem("s_m2")
        s_mean = sem("s_mean")
        s_shift = sem("s_shift")
        s_koff = sem("s_koff")
        s_xn = sem("s_xn")
        s_xg = sem("s_xg")
        s_xsum = sem("s_xsum")
        s_qm = sem("s_qm")
        p_seqT = sem("p_seqT")
        s_seqT = sem("s_seqT")
        p_K = sem("p_K")
        s_K = sem("s_K")
        p_V = sem("p_V")
        s_V = sem("s_V")
        p_koff = sem("p_koff")
        s_koffT = sem("s_koffT")
        p_xT = sem("p_xT")
        s_xT = sem("s_xT")
        p_Q = sem("p_Q")
        s_Q = sem("s_Q")
        p_S = sem("p_S")
        s_S = sem("s_S")
        s_max = sem("s_max")
        s_exp = sem("s_exp")
        s_rec = sem("s_rec")
        s_inv = sem("s_inv")
        s_P = sem("s_P")
        p_PT = sem("p_PT")
        s_PT = sem("s_PT")
        p_z = sem("p_z")
        s_sq = sem("s_sq")
        s_ss = sem("s_ss")
        s_var2 = sem("s_var2")
        s_zn = sem("s_zn")
        p_x2T = sem("p_x2T")
        s_x2T = sem("s_x2T")
        p_H = sem("p_H")
        s_H = sem("s_H")
        p_Y = sem("p_Y")
        s_seq2T = sem("s_seq2T")
        p_seq2 = sem("p_seq2")
        s_seq2 = sem("s_seq2")
        s_ksum2 = sem("s_ksum2")
        s_koff2 = sem("s_koff2")
        c_last = sem("c_last")
        c_pc = sem("c_pc")
        c_cen = sem("c_cen")
        c_sq = sem("c_sq")
        c_pv = sem("c_pv")
        c_var = sem("c_var")
        c_xn = sem("c_xn")
        c_x = sem("c_x")
        c_XL = sem("c_XL")
        c_pq = sem("c_pq")
        c_QB = sem("c_QB")
        c_pa = sem("c_pa")
        c_AB = sem("c_AB")
        c_pk = sem("c_pk")
        c_kT = sem("c_kT")
        c_pS = sem("c_pS")
        c_S = sem("c_S")
        c_max = sem("c_max")
        c_inv = sem("c_inv")
        c_exp = sem("c_exp")
        c_P = sem("c_P")
        c_pPT = sem("c_pPT")
        c_PT = sem("c_PT")
        c_pO = sem("c_pO")
        c_O = sem("c_O")
        c_pOT = sem("c_pOT")
        c_OT = sem("c_OT")

        za = seq[:, 0, 0:QL]
        zc = seq[:, 1, 0:QL]
        zs = seq[:, 2, 0:QL]
        zv = seq[:, 3, 0:QL]
        zr = xn[:, 0, 0:QL]
        zn = xn[:, 1, 0:QL]
        zx = xn[:, 2, 0:QL]
        zh = xn[:, 3, 0:QL]
        zy = att[:, 0, 0:QL]
        zt = x2T[:, 0, 0:QL]
        qml = att[:, 1, 0:QL]
        FT = att[:, 2, :]
        FR = att[:, 3, :]
        f_hi = sb("f_hi", [P, B], BF16)
        f_mid = sb("f_mid", [P, B], BF16)
        f_hl = sb("f_hl", [P, B], BF16)
        NB = 500
        NC = 1000
        CH = NITEMS // NC
        NT = B // P
        it32 = [emb[0:D, 2 * i:2 * i + 2, :].rearrange("p a b -> p (a b)")[:, 0:NC] for i in range(2)]
        irem = xg[0:D, 0:2, :].rearrange("p a b -> p (a b)")[:, 0:NC]
        imid = sb("imid", [D, NC], BF16)
        SLOTS = 4
        ix = [sb(f"ix{i}", [P, NC], BF16) for i in range(SLOTS)]
        iy = [sb(f"iy{i}", [P, NC], BF16) for i in range(SLOTS)]
        AHEAD = 3
        FIRST = 2
        ROUNDS = (CH - FIRST - AHEAD) // SLOTS
        assert CH * NC == NITEMS and FIRST + AHEAD + ROUNDS * SLOTS == CH and CH % 2 == 1
        ost = [(KT, V, QT, HT)[i][:, 2 * k:2 * k + 2, :].rearrange("p a b -> p (a b)")[:, 0:NC]
               for k in range(2) for i in range(4)]
        e_pe = sem("e_pe")
        e_dve = sem("e_dve")
        e_act = sem("e_act")
        RSQRT = 11
        E_SUM = 3
        E_CENTRED = E_SUM + 1
        E_VAR = E_CENTRED + 1
        E_NORMED = E_VAR + 6
        E_OUT = E_NORMED + 2
        E_CENTRED2 = E_OUT + 1
        E_VAR2 = E_CENTRED2 + 1
        E_NORMED2 = E_VAR2 + 6
        f_split = sem("f_split")
        i_load = [sem(f"i_load{i}") for i in range(2)]
        i_hi = sem("i_hi")
        i_rem = sem("i_rem")
        i_mid = sem("i_mid")
        i_hs = sem("i_hs")
        i_xy = sem("i_xy")
        i_mm = sem("i_mm")
        o_even = sem("o_even")
        o_odd = sem("o_odd")
        o_st = [sem(f"o_st{i}") for i in range(2)]

        block = ctx.enter_context(nc.Block())

        def v1(c, h=None):
            return vec[:, c:c + 1] if h is None else vec[D * h:D * h + D, c:c + 1]

        def tiles(buf, u):
            return buf[:, u, :].rearrange("p (t f) -> p t f", f=D)

        def spread(small):
            return small.unsqueeze(2).broadcast_to([P, T, D])

        gain_b = gain_row[:, :].unsqueeze(1).broadcast_to([P, T, D])
        pos_b = pos2[:, :].unsqueeze(1).broadcast_to([P, T, D])
        DVE_SUMS = 2
        DVE_GAINS = 3

        def summed(eng, i, u):
            if isinstance(i, int) and i < DVE_SUMS:
                eng.wait_ge(s_raw_dve, i * U + u + 1)
            else:
                eng.wait_ge(s_raw, (i - DVE_SUMS) * U + u + 1)

        def multiplied(eng, i, u):
            if isinstance(i, int) and i < DVE_GAINS:
                eng.wait_ge(s_xg_dve, i * U + u + 1)
            else:
                eng.wait_ge(s_xg, (i - DVE_GAINS) * U + u + 1)

        n_const = [0]
        n_prep = [0]

        @block.sync
        def _(sp):
            def load(dst, src):
                sp.dma_start(dst, src).then_inc(s_const, 16)
                n_const[0] += 16
            sp.dma_start(ids_i[:, :], ids_tok).then_inc(s_ids, 16)
            for h in range(2):
                load(idl_i[D * h:D * h + D, :], ids_last[h:h + 1, :].broadcast_to([D, QL]))
            load(ident[:, :], ident_c)
            load(center[:, :], center_c)
            load(mean_m[:, :], mean_c)
            load(causal[:, :], causal_c)
            load(diag2[:, :], diag2_c)
            load(sel1f, sel1_c)
            load(sel2f, sel2_c)
            for h in range(2):
                load(vec[D * h:D * h + D, :], vecs)
                load(pos2[D * h:D * h + D, :], pos)
            load(bvr[:, :], bv_row.broadcast_to([P, D]))
            load(gain_row[:, :], ln_rows[0:1, :].broadcast_to([P, D]))
            load(bias_row[:, :], ln_rows[1:2, :].broadcast_to([P, D]))
            sp.wait_ge(s_zero, 1)
            for h in range(2):
                load(wbd[D * h:D * h + D, :, D * h:D * h + D], weights)

            def store(c, k):
                for t in range(NT):
                    sp.wait_ge(o_even, (c * NT + t) + 1)
                    sp.wait_ge(o_odd, (c * NT + t) + 1)
                    sp.dma_start(out[P * t:P * t + P, bass.ds(c * NC, NC)],
                                 ost[k * NT + t]).then_inc(o_st[k], 16)

            with sp.Fori(0, CH // 2) as c2:
                store(c2 * 2, 0)
                store(c2 * 2 + 1, 1)
            store(CH - 1, 0)
            for k in range(2):
                sp.wait_ge(o_st[k], 16 * NT * ((CH + 1 - k) // 2))

        @block.gpsimd
        def _(pool):
            pool.memset(wbd[:, :, :], 0.0).then_inc(s_zero, 1)
            pool.memset(QB[:, :, :], 0.0).then_inc(s_zero, 1)

            def gather(i, u):
                if u == 0:
                    if not isinstance(i, int) or i > 0:
                        for v in range(U):
                            pool.wait_ge(s_gath[v], i * (16 * T))
                    pool.tensor_copy(idx_now[:, :], idx[:, bass.ds(i * (U * T), U * T)]).then_inc(s_now, 1)
                    pool.wait_ge(s_now, i + 1)
                if not isinstance(i, int) or i > 0:
                    summed(pool, i - 1, u)
                pool.sem_inc(s_room, 1)
                for t in range(T):
                    pool.indirect_dma_start(
                        out=emb[:, u, D * t:D * t + D], out_offset=None, in_=item_emb,
                        in_offset=bass.IndirectOffsetOnAxis(ap=idx_now[:, u * T + t:u * T + t + 1], axis=0),
                    ).then_inc(s_gath[u], 16)

            pool.wait_ge(s_idx, 1)
            pool.wait_ge(s_zero, 2)

            def gained(i):
                for u in range(U):
                    if not isinstance(i, int) or i > 0:
                        pool.wait_ge(s_xsum, (i - 1) * U + u + 1)
                    pool.wait_ge(s_xn, i * U + u + 1)
                    pool.tensor_tensor(tiles(xg, u), tiles(xn, u), gain_b, ALU.mult).then_inc(s_xg, 1)

            def placed(i, u):
                if not isinstance(i, int) or i > 0:
                    pool.wait_ge(s_seq, (i - 1) * U + u + 1)
                pool.wait_ge(s_gath[u], (i + 1) * (16 * T))
                pool.tensor_tensor(tiles(placed_emb, u), tiles(emb, u), pos_b, ALU.add).then_inc(s_raw, 1)

            for i in range(DVE_SUMS):
                for u in range(U):
                    gather(i, u)
            pool.wait_ge(s_const, n_const[0])
            for i in (2, 3, 4):
                for u in range(U):
                    gather(i, u)
                for u in range(U):
                    placed(i, u)
            gained(3)
            with pool.Fori(5, STEPS) as i:
                for u in range(U):
                    gather(i, u)
                for u in range(U):
                    placed(i, u)
                gained(i - 1)
            gained(STEPS - 1)

            def load_items(c, k, first=False):
                if not first:
                    pool.wait_ge(i_hi, c - 1)
                    pool.wait_ge(i_rem, c - 1)
                pool.dma_start(it32[k], items_t[:, bass.ds(c * NC, NC)]).then_inc(i_load[k], 16)

            pool.wait_ge(s_raw, (STEPS - DVE_SUMS) * U)
            load_items(0, 0, True)
            load_items(1, 1, True)
            with pool.Fori(1, CH // 2) as c2:
                load_items(c2 * 2, 0)
                load_items(c2 * 2 + 1, 1)
            load_items(CH - 1, 0)

        @block.vector
        def _(dve):
            def prep(ins):
                n_prep[0] += 1
                ins.then_inc(s_prep, 1)
                dve.wait_ge(s_prep, n_prep[0])

            dve.wait_ge(s_ids, 16)
            prep(dve.tensor_copy(ids_f[:, :], ids_i[:, :]))
            prep(dve.tensor_scalar(mask[:, :], ids_f[:, :], float(NROW - 1), None, ALU.not_equal))
            prep(dve.tensor_scalar(ids_n[:, :], ids_f[:, :], 0.0, float(NROW), ALU.is_lt, ALU.mult))
            prep(dve.tensor_tensor(ids_f[:, :], ids_f[:, :], ids_n[:, :], ALU.add))
            prep(dve.tensor_scalar(ids_f[:, :], ids_f[:, :], 0.0, float(NROW - 1), ALU.max, ALU.min))
            dve.tensor_copy(idx[:, :], ids_f[:, :]).then_inc(s_idx, 1)
            dve.wait_ge(s_const, n_const[0])
            prep(dve.tensor_scalar(mlast[:, :], idl_i[:, :], float(NROW - 1), None, ALU.not_equal))
            prep(dve.tensor_copy(sel1[:, :], sel1f))
            prep(dve.tensor_copy(sel2[:, :], sel2f))
            prep(dve.tensor_scalar(vec8[:, 0:1], v1(BQ0), 0.125, None, ALU.mult))
            prep(dve.tensor_scalar(vec8[:, 1:2], v1(BQ1), 0.125, None, ALU.mult))
            for h in range(2):
                a, b = D * h, D * h + D
                blk = wbd[a:b, WV0, a:b]
                prep(dve.tensor_reduce(wmean[a:b, 0:1], blk, AX.X, ALU.add))
                prep(dve.tensor_scalar(wmean[a:b, 1:2], wmean[a:b, 0:1], 1.0 / D, None, ALU.mult))
                prep(dve.tensor_scalar(blk, blk, wmean[a:b, 1:2], None, ALU.subtract))
            prep(dve.tensor_reduce(wmean[:, 4:5], bias_row[:, :], AX.X, ALU.add))
            prep(dve.tensor_reduce(wmean[:, 2:3], bvr[:, :], AX.X, ALU.add))
            prep(dve.tensor_scalar(wmean[:, 3:4], wmean[:, 2:3], 1.0 / D, None, ALU.mult))
            prep(dve.tensor_scalar(bvr[:, :], bvr[:, :], wmean[:, 3:4], None, ALU.subtract))
            prep(dve.tensor_copy(bv3[:, 0, :], bvr[:, :]))
            prep(dve.tensor_tensor(bvr[:, :], bvr[:, :], bv3[:, 0, :], ALU.subtract))
            prep(dve.tensor_copy(bv3[:, 1, :], bvr[:, :]))
            prep(dve.tensor_tensor(bvr[:, :], bvr[:, :], bv3[:, 1, :], ALU.subtract))
            prep(dve.tensor_copy(bv3[:, 2, :], bvr[:, :]))
            rows = bv_rows[:, :].rearrange("p (t f) -> p t f", f=D)
            part = [bv3[:, k, :].unsqueeze(1).broadcast_to([P, T, D]) for k in range(3)]
            prep(dve.tensor_scalar(rows, part[0], ident[:, 0:1], None, ALU.mult))
            for k in (1, 2):
                prep(dve.scalar_tensor_tensor(out=rows, in0=part[k], scalar=ident[:, k:k + 1], in1=rows,
                                              op0=ALU.mult, op1=ALU.add))
            prep(dve.memset(ones3[:, :], 1.0))
            prep(dve.memset(bkrep[:, :], 0.0))
            prep(dve.tensor_scalar(bkrep[:, :], bkrep[:, :], v1(BK1), None, ALU.add))

            causal_b = causal[:, :].unsqueeze(1).broadcast_to([P, T, D])

            def rsqrt_chain(n, rows):
                k = [0]

                def step(ins):
                    k[0] += 1
                    ins.then_inc(s_rsq, 1)
                    dve.wait_ge(s_rsq, n * RSQRT + k[0])

                def rows_of(first):
                    return st[:, first + rows[0]:first + rows[1], :, :].rearrange("p k u t -> p (k u t)")

                rsqrt_steps(step, rows_of(VAR), rows_of(RSTD), rows_of(TMP))

            def rsqrt_steps(step, v, y, t):
                step(dve.tensor_scalar(y.bitcast(I32), v.bitcast(I32), 1, None, ALU.logical_shift_right))
                step(dve.tensor_scalar(y.bitcast(I32), y.bitcast(I32), -1.0, RSQRT_MAGIC, ALU.mult, ALU.add))
                for _ in range(3):
                    step(dve.tensor_tensor(t, v, y, ALU.mult))
                    step(dve.scalar_tensor_tensor(out=t, in0=t, scalar=-0.5, in1=y, op0=ALU.mult, op1=ALU.mult))
                    step(dve.scalar_tensor_tensor(out=y, in0=t, scalar=1.5, in1=y, op0=ALU.add, op1=ALU.mult))

            def uses(i):
                return (0, 2, 3, 5)[i] if isinstance(i, int) and i < 4 else i + 3

            def flat(k):
                return st[:, k, :, :].rearrange("p u t -> p (u t)")

            def pre_seq(i):
                for u in range(U):
                    n = i * U + u
                    m = mask[:, bass.ds(n * T, T)]
                    if not isinstance(i, int) or i > 0:
                        dve.wait_ge(p_seqT, (i - 1) * U + u + 1)
                    if isinstance(i, int) and i < DVE_SUMS:
                        dve.wait_ge(s_gath[u], (i + 1) * (16 * T))
                        dve.tensor_tensor(tiles(placed_emb, u), tiles(emb, u), pos_b, ALU.add).then_inc(s_raw_dve, 1)
                    summed(dve, i, u)
                    dve.tensor_tensor(tiles(seq, u), tiles(placed_emb, u), spread(m), ALU.mult).then_inc(s_seq, 1)

            def pre_bn(i, u):
                dve.wait_ge(s_seq, i * U + u + 1)
                for t in range(T):
                    last = dve.bn_stats(stat[:, u, t, :], seq[:, u, D * t:D * t + D])
                last.then_inc(s_stat, 1)

            def pre_var(i):
                dve.wait_ge(s_stat, i * U + U)
                me, Me = stat[:, :, :, 1], stat[:, :, :, 2]
                mo, Mo = stat[:, :, :, 4], stat[:, :, :, 5]
                dve.tensor_tensor(st[:, DIF, :, :], me, mo, ALU.subtract).then_inc(s_dif, 1)
                dve.tensor_tensor(st[:, SUM, :, :], me, mo, ALU.add).then_inc(s_sum, 1)
                dve.wait_ge(s_dif, 2 * i + 1)
                dve.tensor_tensor(flat(DIF), flat(DIF), flat(DIF), ALU.mult).then_inc(s_dif, 1)
                dve.tensor_tensor(st[:, TMP, :, :], Me, Mo, ALU.add).then_inc(s_m2, 1)
                dve.wait_ge(s_sum, i + 1)
                dve.tensor_scalar(flat(MEAN), flat(SUM), 0.5, None, ALU.mult).then_inc(s_mean, 1)
                dve.wait_ge(s_dif, 2 * i + 2)
                dve.wait_ge(s_m2, 2 * i + 1)
                dve.scalar_tensor_tensor(out=flat(TMP), in0=flat(DIF), scalar=D / 4.0, in1=flat(TMP),
                                         op0=ALU.mult, op1=ALU.add).then_inc(s_m2, 1)
                dve.wait_ge(s_m2, 2 * i + 2)
                dve.tensor_scalar(flat(VAR), flat(TMP), 1.0 / D, EPS, ALU.mult, ALU.add).then_inc(s_var, 1)
                dve.wait_ge(s_var, i + 1)

            def pre_norm(i):
                dve.wait_ge(s_mean, i + 1)
                for u in range(U):
                    n = i * U + u
                    if not isinstance(i, int) or i > 0:
                        dve.wait_ge(p_xT, (i - 1) * U + u + 1)
                        multiplied(dve, i - 1, u)
                    dve.tensor_tensor(tiles(xn, u), tiles(seq, u), spread(st[:, MEAN, u, :]),
                                      ALU.subtract).then_inc(s_shift, 1)
                    dve.wait_ge(s_shift, n + 1)
                    dve.tensor_tensor(tiles(xn, u), tiles(xn, u), spread(st[:, RSTD, u, :]),
                                      ALU.mult).then_inc(s_xn, 1)
                dve.tensor_scalar(koff[:, :], flat(SUM), 0.0, KEY_OFF, ALU.is_equal, ALU.mult).then_inc(s_koff, 1)

            def front_qmask(i):
                for u in range(U):
                    if isinstance(i, int) and i < DVE_GAINS:
                        dve.wait_ge(s_xn, i * U + u + 1)
                        dve.tensor_tensor(tiles(xg, u), tiles(xn, u), gain_b, ALU.mult).then_inc(s_xg_dve, 1)
                    multiplied(dve, i, u)
                    dve.tensor_reduce(st[:, XSUM, u, :], tiles(xg, u), AX.X, ALU.add).then_inc(s_xsum, 1)
                dve.wait_ge(s_xsum, i * U + U)
                nat = st[:, XSUM, :, :].rearrange("p u (j h) -> p (u j) h", h=2)
                scl = st[:, QMASK, :, :].rearrange("p u (j s) -> p (u j) s", s=2)
                for h in range(2):
                    for s in range(2):
                        last = dve.tensor_scalar(scl[D * h:D * h + D, :, s], nat[D * s:D * s + D, :, h],
                                                 wmean[D * s:D * s + D, 4:5], 0.0, ALU.add, ALU.not_equal)
                last.then_inc(s_qm, 1)

            def front_scores(i, u):
                n = i * U + u
                dve.wait_ge(p_S, n + 1)
                if not isinstance(i, int) or i > 0:
                    dve.wait_ge(p_PT, (i - 1) * U + u + 1)
                sc = front[u][:, :].rearrange("p (t k) -> p t k", k=D)
                dve.scalar_tensor_tensor(out=tiles(att, u), in0=sc, scalar=NEG, in1=causal_b,
                                         op0=ALU.max, op1=ALU.min).then_inc(s_S, 1)
                dve.wait_ge(s_S, n + 1)
                dve.tensor_reduce(st[:, NMAX, u, :], tiles(att, u), AX.X, ALU.max,
                                  negate=True).then_inc(s_max, 1)

            def front_norm(i, u):
                n = i * U + u
                dve.wait_ge(s_exp, n + 1)
                dve.reciprocal(st[:, INV, u, :], st[:, ESUM, u, :]).then_inc(s_rec, 1)
                dve.wait_ge(s_rec, n + 1)
                dve.wait_ge(s_qm, i + 1)
                dve.tensor_tensor(st[:, INV, u, :], st[:, INV, u, :], st[:, QMASK, u, :],
                                  ALU.mult).then_inc(s_inv, 1)
                dve.wait_ge(s_inv, n + 1)
                dve.tensor_tensor(tiles(att, u), tiles(att, u), spread(st[:, INV, u, :]),
                                  ALU.mult).then_inc(s_P, 1)

            def back_square_sum(i, u):
                dve.wait_ge(s_sq, i * U + u + 1)
                dve.tensor_reduce(st[:, SQ, u, :], tiles(zq, u), AX.X, ALU.add).then_inc(s_ss, 1)

            def back_var(i):
                dve.wait_ge(s_ss, i * U + U)
                dve.tensor_scalar(flat(VAR2), flat(SQ), 1.0 / D, EPS, ALU.mult, ALU.add).then_inc(s_var2, 1)
                dve.wait_ge(s_var2, i + 1)

            def back_norm(i):
                for u in range(U):
                    z = back(0, u)[:, :].rearrange("p (t f) -> p t f", f=D)
                    dve.tensor_tensor(tiles(zq, u), z, spread(st[:, RSTD2, u, :]), ALU.mult).then_inc(s_zn, 1)

            def back_out(i, u):
                if not isinstance(i, int) or i > 0:
                    dve.wait_ge(c_pS, i)
                dve.wait_ge(p_Y, i * U + u + 1)
                dve.scalar_tensor_tensor(out=seq2T[:, u, :], in0=back(3, u)[:, :], scalar=v1(B20),
                                         in1=x2T[:, u, :], op0=ALU.add, op1=ALU.add).then_inc(s_seq2T, 1)

            def last_columns(i):
                dve.wait_ge(s_seq2T, i * U + U)
                cols = seq2T[:, :, :].rearrange("p u (c q) -> p u c q", q=D)[:, :, :, D - 1]
                dve.tensor_tensor(xl[:, 0, :].rearrange("p (u c) -> p u c", u=U), cols,
                                  mlast[:, bass.ds(i * LC, LC)].rearrange("p (u c) -> p u c", u=U),
                                  ALU.mult).then_inc(c_last, 1)

            def back_tokens(i, groups):
                for u in groups:
                    n = i * U + u
                    if not isinstance(i, int) or i > 0:
                        dve.wait_ge(c_pO, i)
                    dve.wait_ge(p_seq2, n + 1)
                    m = mask[:, bass.ds(n * T, T)]
                    dve.tensor_tensor(tiles(seq2, u), back(4, u)[:, :].rearrange("p (t f) -> p t f", f=D),
                                      spread(m), ALU.mult).then_inc(s_seq2, 1)

            def back_key_mask(i):
                for u in range(U):
                    dve.wait_ge(s_seq2, i * U + u + 1)
                    last = dve.tensor_reduce(st[:, KSUM, u, :], tiles(seq2, u), AX.X, ALU.add)
                last.then_inc(s_ksum2, 1)
                dve.wait_ge(s_ksum2, i + 1)
                dve.tensor_scalar(koff2[:, :], flat(KSUM), 0.0, KEY_OFF,
                                  ALU.is_equal, ALU.mult).then_inc(s_koff2, 1)

            def last_centre(i):
                dve.wait_ge(c_pc, i + 1)
                dve.tensor_copy(xl[:, 1, :], spare[:, 0:LC]).then_inc(c_cen, 1)
                dve.wait_ge(c_cen, i + 1)
                dve.tensor_tensor(xl[:, 2, :], xl[:, 1, :], xl[:, 1, :], ALU.mult).then_inc(c_sq, 1)

            def last_var(i):
                dve.wait_ge(c_pv, i + 1)
                dve.tensor_scalar(flat(VARL), spare[:, 0:LC], EPS, None, ALU.add).then_inc(c_var, 1)
                dve.wait_ge(c_var, i + 1)

            def last_norm(i):
                dve.tensor_tensor(xl[:, 5, :], xl[:, 1, :], flat(RSTDL), ALU.mult).then_inc(c_xn, 1)

            def last_scores(i):
                dve.wait_ge(c_pS, i + 1)
                dve.scalar_tensor_tensor(out=s2[:, :], in0=spare[:, :], scalar=NEG, in1=diag2[:, :],
                                         op0=ALU.max, op1=ALU.min).then_inc(c_S, 1)
                dve.wait_ge(c_S, i + 1)
                dve.tensor_reduce(s2v[:, 0:1], s2[:, :], AX.X, ALU.max, negate=True).then_inc(c_max, 1)

            def last_probs(i):
                dve.wait_ge(c_exp, i + 1)
                dve.reciprocal(s2v[:, 2:3], s2v[:, 1:2]).then_inc(c_inv, 1)
                dve.wait_ge(c_inv, i + 1)
                dve.tensor_scalar(s2[:, :], s2[:, :], s2v[:, 2:3], None, ALU.mult).then_inc(c_P, 1)

            def last_attended(i):
                dve.wait_ge(c_pO, i + 1)
                dve.tensor_copy(o2[:, :], spare[:, 0:P]).then_inc(c_O, 1)

            def last_store(i):
                dve.wait_ge(c_pOT, i + 1)
                src = spare[:, 0:P].rearrange("p (u m) -> p u m", u=U)
                for h in range(2):
                    a, b = D * h, D * h + D
                    last = dve.tensor_copy(OT[a:b, bass.ds(i * LC, LC)].rearrange("p (u c) -> p u c", u=U),
                                           src[a:b, :, 2 * J * h:2 * J * h + 2 * J])
                last.then_inc(c_OT, 1)

            def pre(i):
                pre_seq(i)
                for u in range(U):
                    pre_bn(i, u)
                pre_var(i)
                rsqrt_chain((0, 1, None, 4, 6)[i], (0, 1))
                pre_norm(i)

            def split(c, slot):
                dve.wait_ge(i_hi, c + 1)
                if not isinstance(c, int) or c > 0:
                    dve.wait_ge(i_xy, c)
                dve.tensor_tensor(irem, it32[0 if slot % 2 == 0 else 1], ix[slot][0:D, :],
                                  ALU.subtract).then_inc(i_rem, 1)
                dve.wait_ge(i_rem, c + 1)
                dve.tensor_copy(imid[:, :], irem).then_inc(i_mid, 1)
                dve.wait_ge(i_mid, c + 1)
                dve.tensor_copy(ix[slot][D:P, :], imid[:, :])
                dve.tensor_tensor(iy[slot][0:D, :], irem, imid[:, :], ALU.subtract).then_inc(i_xy, 1)

            NONE, EARLY, MIDDLE, LATE, ROWS_LATE = range(5)

            def body(i, when, a, b, c):
                p = when == EARLY
                own = isinstance(i, int) and i == 2
                if c:
                    back_key_mask(i - 2)
                    last_var(i - 2)
                if p:
                    pre_seq(i + 1)
                    pre_bn(i + 1, 0)
                for u in range(U - 1):
                    if p:
                        pre_bn(i + 1, u + 1)
                    if b:
                        back_square_sum(i - 1, u)
                if p:
                    pre_var(i + 1)
                if own:
                    pre_var(i)
                if b:
                    back_square_sum(i - 1, U - 1)
                    back_var(i - 1)
                if p or b or c:
                    rsqrt_chain(uses(i), (0 if p or own else 1 if b else 2, 3 if c else 2 if b else 1))
                if c:
                    last_norm(i - 2)
                if c and not b:
                    split(0, 0)
                    split(1, 1)
                if b:
                    back_norm(i - 1)
                if own:
                    pre_norm(i)
                if a:
                    front_qmask(i)
                if p:
                    pre_norm(i + 1)
                if when == MIDDLE:
                    pre(i + 1)
                if c:
                    last_scores(i - 2)
                for u in range(U):
                    if a:
                        front_scores(i, u)
                    if u == 0 and c:
                        last_probs(i - 2)
                    if b:
                        back_out(i - 1, u)
                    if u >= 2 and a:
                        front_norm(i, u - 2)
                if b:
                    last_columns(i - 1)
                if c:
                    last_attended(i - 2)
                    last_store(i - 2)
                if a:
                    front_norm(i, 2)
                if b:
                    back_tokens(i - 1, (0,))
                if a:
                    front_norm(i, 3)
                if when == LATE:
                    pre(i + 1)
                if when == ROWS_LATE:
                    pre_seq(i + 1)
                if b:
                    back_tokens(i - 1, (1,))
                    last_centre(i - 1)
                    back_tokens(i - 1, (2, 3))
                if when == ROWS_LATE:
                    for u in range(U):
                        pre_bn(i + 1, u)

            pre(0)
            body(0, LATE, True, False, False)
            body(1, ROWS_LATE, True, True, False)
            body(2, MIDDLE, True, True, True)
            body(3, MIDDLE, True, True, True)
            with dve.Fori(4, STEPS - 1) as i:
                body(i, EARLY, True, True, True)
            body(STEPS - 1, NONE, True, True, True)
            body(STEPS, NONE, False, True, True)

            def drain_even(c, k, free=None):
                if free is not None:
                    dve.wait_ge(o_st[k], free)
                for t in range(NT):
                    dve.wait_ge(i_mm, c * NT * 2 + 2 * t + 1)
                    dve.tensor_copy(ost[k * NT + t][:, 0:NB], banks[2 * t][:, 0:NB]).then_inc(o_even, 1)

            body(STEPS + 1, NONE, False, False, True)

            own_no = [0]

            def own(ins):
                own_no[0] += 1
                ins.then_inc(e_dve, 1)
                dve.wait_ge(e_dve, own_no[0])

            def norm_own(bank, root):
                own(dve.tensor_scalar(zv, bank[:, 0:QL], EPS, None, ALU.add))
                dve.wait_ge(e_act, root)
                own(dve.reciprocal(zr, zr))
                own(dve.tensor_tensor(zt, zv, zr, ALU.mult))
                own(dve.tensor_tensor(zt, zt, zr, ALU.mult))
                own(dve.tensor_scalar(zt, zt, -0.5, 1.5, ALU.mult, ALU.add))
                own(dve.tensor_tensor(zr, zr, zt, ALU.mult))
                own(dve.tensor_tensor(zn, zc, zr, ALU.mult))

            dve.wait_ge(e_pe, 1)
            own(dve.tensor_scalar(qml, hi[1][:, 0:QL], 0.0, None, ALU.not_equal))
            dve.wait_ge(e_pe, 2)
            own(dve.scalar_tensor_tensor(out=za, in0=hi[0][:, 0:QL], scalar=v1(BV1), in1=qml,
                                         op0=ALU.add, op1=ALU.mult))
            own(dve.tensor_tensor(za, za, XL[:, :], ALU.add))
            assert own_no[0] == E_SUM
            dve.wait_ge(e_pe, 3)
            own(dve.tensor_copy(zc, lo[0][:, 0:QL]))
            assert own_no[0] == E_CENTRED
            dve.wait_ge(e_pe, 4)
            norm_own(lo[1], 2)
            assert own_no[0] == E_NORMED
            dve.wait_ge(e_act, 3)
            dve.wait_ge(e_pe, 6)
            own(dve.scalar_tensor_tensor(out=zy, in0=lo[3][:, 0:QL], scalar=v1(B21), in1=zx,
                                         op0=ALU.add, op1=ALU.add))
            own(dve.tensor_tensor(zy, zy, mlast[:, :], ALU.mult))
            assert own_no[0] == E_OUT
            dve.wait_ge(e_pe, 7)
            own(dve.tensor_copy(zc, hi[2][:, 0:QL]))
            assert own_no[0] == E_CENTRED2
            dve.wait_ge(e_pe, 8)
            norm_own(hi[3], 6)
            assert own_no[0] == E_NORMED2
            dve.wait_ge(e_act, 7)
            ftv = FT.rearrange("p (g h s) -> p g h s", h=2, s=2)
            zxv = zx.rearrange("p (g s) -> p g s", s=2)
            for dup in range(2):
                for h in range(2):
                    last = dve.tensor_copy(ftv[D * dup:D * dup + D, :, h, :], zxv[D * h:D * h + D, :, :])
            own(last)
            own(dve.tensor_copy(f_hi[:, :], FT))
            dve.tensor_copy(f_hl[0:D, :], f_hi[0:D, :])
            own(dve.tensor_tensor(FR, FT, f_hi[:, :], ALU.subtract))
            own(dve.tensor_copy(f_mid[:, :], FR))
            dve.tensor_tensor(f_hl[D:P, :], FR[D:P, :], f_mid[D:P, :], ALU.subtract).then_inc(f_split, 1)

            split(2, 2)
            for c in range(FIRST):
                split(c + AHEAD, (c + AHEAD) % SLOTS)
                drain_even(c, c)
            with dve.Fori(0, ROUNDS) as rd:
                for q in range(SLOTS):
                    c = rd * SLOTS + (FIRST + q)
                    split(c + AHEAD, (FIRST + q + AHEAD) % SLOTS)
                    drain_even(c, q % 2, (rd * (SLOTS // 2) + (FIRST + q) // 2) * (16 * NT))
            for c in range(CH - AHEAD, CH):
                drain_even(c, c % 2, (c // 2) * (16 * NT))

        @block.scalar
        def _(act):
            def front_copy(i, out, p_sem, s_sem, func=ACT.Copy, **kw):
                for u in range(U):
                    act.wait_ge(p_sem, i * U + u + 1)
                    act.activation(out[:, u, :], front[u][:, :], func, **kw).then_inc(s_sem, 1)

            def front_values(i):
                for u in range(U):
                    if not isinstance(i, int) or i > 0:
                        act.wait_ge(p_z, (i - 1) * U + u + 1)
                    act.wait_ge(p_V, i * U + u + 1)
                    act.activation(V[:, u, :], front[u][:, :], ACT.Copy).then_inc(s_V, 1)

            def front_koffT(i):
                act.wait_ge(p_koff, i + 1)
                act.activation(koffT[:, :], front[0][0:U * T, 0:P], ACT.Copy).then_inc(s_koffT, 1)

            def front_exp(i, groups):
                for u in groups:
                    act.wait_ge(s_max, i * U + u + 1)
                    for t in range(T):
                        blk = att[:, u, D * t:D * t + D]
                        last = act.activation(blk, blk, ACT.Exp, bias=st[:, NMAX, u, t:t + 1],
                                              accum_out=st[:, ESUM, u, t:t + 1])
                    last.then_inc(s_exp, 1)

            def back_copy(i, k, out, p_sem, s_sem, func, groups=range(U), **kw):
                for u in groups:
                    act.wait_ge(p_sem, i * U + u + 1)
                    act.activation(out[:, u, :], back(k, u)[:, :], func, **kw).then_inc(s_sem, 1)

            def last_keys(i):
                act.wait_ge(c_pk, i + 1)
                act.activation(koffT2[:, :], spare[0:U * T, 0:P], ACT.Copy).then_inc(c_kT, 1)

            def last_affine(i):
                act.wait_ge(c_xn, i + 1)
                act.activation(xl[:, 7, :], xl[:, 5, :], ACT.Identity, bias=v1(LN1B1),
                               scale=v1(LN1G1)).then_inc(c_x, 1)

            def last_keep(i):
                act.activation(XL[:, bass.ds(i * LC, LC)], xl[:, 5, :], ACT.Identity, bias=v1(LN1B1),
                               scale=v1(LN1G1)).then_inc(c_XL, 1)

            def last_query(i):
                act.wait_ge(c_pq, i + 1)
                for h in range(2):
                    a, b = D * h, D * h + D
                    last = act.activation(QB[a:b, :, 2 * J * h:2 * J * h + 2 * J],
                                          spare[a:b, 0:LC].rearrange("p (u c) -> p u c", u=U), ACT.Identity,
                                          bias=vec8[a:b, 1:2], scale=0.125)
                last.then_inc(c_QB, 1)

            def last_weighted(i):
                act.wait_ge(c_pa, i + 1)
                act.activation(AB[:, :, :].rearrange("p u c -> p (u c)"), spare[:, 0:P],
                               ACT.Copy).then_inc(c_AB, 1)

            def last_exp(i):
                act.wait_ge(c_max, i + 1)
                act.activation(s2[:, :], s2[:, :], ACT.Exp, bias=s2v[:, 0:1],
                               accum_out=s2v[:, 1:2]).then_inc(c_exp, 1)

            def last_turned(i):
                act.wait_ge(c_pPT, i + 1)
                act.activation(PT2[:, :], spare[:, :], ACT.Copy).then_inc(c_PT, 1)

            def body(i, a, b, c):
                if a:
                    front_copy(i, seqT, p_seqT, s_seqT)
                if b:
                    back_copy(i - 1, 0, zq, p_z, s_sq, ACT.Square)
                if a:
                    front_copy(i, KT, p_K, s_K, ACT.Identity, bias=v1(BK0))
                    front_values(i)
                    front_koffT(i)
                if c:
                    last_affine(i - 2)
                if b:
                    back_copy(i - 1, 1, x2T, p_x2T, s_x2T, ACT.Identity, bias=v1(LN2B0), scale=v1(LN2G0))
                if c:
                    last_query(i - 2)
                    last_keep(i - 2)
                if a:
                    front_copy(i, xT, p_xT, s_xT, ACT.Identity, bias=v1(LN1B0), scale=v1(LN1G0))
                if c:
                    last_weighted(i - 2)
                if b:
                    back_copy(i - 1, 2, HT, p_H, s_H, ACT.Relu, bias=v1(B10))
                if c:
                    last_keys(i - 2)
                if a:
                    front_copy(i, QT, p_Q, s_Q, ACT.Identity, bias=vec8[:, 0:1], scale=0.125)
                if c:
                    last_exp(i - 2)
                if a:
                    front_exp(i, (0, 1))
                if c:
                    last_turned(i - 2)
                if a:
                    front_exp(i, (2, 3))
                    front_copy(i, PT, p_PT, s_PT)

            body(0, True, False, False)
            body(1, True, True, False)
            with act.Fori(2, STEPS) as i:
                body(i, True, True, True)
            body(STEPS, False, True, True)

            def high(c, slot, loads):
                act.wait_ge(i_load[slot % 2], loads * 16)
                if not isinstance(c, int) or c >= SLOTS:
                    act.wait_ge(i_mm, (c - (SLOTS - 1)) * (2 * NT))
                act.activation(ix[slot][0:D, :], it32[slot % 2], ACT.Copy).then_inc(i_hi, 1)
                act.wait_ge(i_hi, c + 1)
                act.activation(iy[slot][D:P, :], ix[slot][0:D, :], ACT.Copy).then_inc(i_hs, 1)

            def drain_odd(c, k, free=None):
                if free is not None:
                    act.wait_ge(o_st[k], free)
                for t in range(NT):
                    act.wait_ge(i_mm, c * NT * 2 + 2 * t + 2)
                    act.activation(ost[k * NT + t][:, NB:NC], banks[2 * t + 1][:, 0:NB],
                                   ACT.Copy).then_inc(o_odd, 1)

            high(0, 0, 1)
            high(1, 1, 1)
            body(STEPS + 1, False, False, True)

            act.wait_ge(e_dve, E_CENTRED)
            act.activation(zs, lo[0][:, 0:QL], ACT.Square).then_inc(e_act, 1)
            act.wait_ge(e_dve, E_VAR)
            act.activation(zr, zv, ACT.Sqrt).then_inc(e_act, 1)
            act.wait_ge(e_dve, E_NORMED)
            act.activation(zx, zn, ACT.Identity, bias=v1(LN2B1), scale=v1(LN2G1)).then_inc(e_act, 1)
            act.wait_ge(e_pe, 5)
            act.activation(zh, lo[2][:, 0:QL], ACT.Relu, bias=v1(B11)).then_inc(e_act, 1)
            act.wait_ge(e_dve, E_CENTRED2)
            act.activation(zs, hi[2][:, 0:QL], ACT.Square).then_inc(e_act, 1)
            act.wait_ge(e_dve, E_VAR2)
            act.activation(zr, zv, ACT.Sqrt).then_inc(e_act, 1)
            act.wait_ge(e_dve, E_NORMED2)
            act.activation(zx, zn, ACT.Identity, bias=v1(LNFB), scale=v1(LNFG)).then_inc(e_act, 1)

            for c in range(2, FIRST + AHEAD):
                high(c, c % SLOTS, c // 2 + 1)
                if c >= AHEAD:
                    drain_odd(c - AHEAD, c - AHEAD)
            with act.Fori(0, ROUNDS) as rd:
                for q in range(SLOTS):
                    c = rd * SLOTS + (FIRST + q)
                    high(c + AHEAD, (FIRST + q + AHEAD) % SLOTS, rd * (SLOTS // 2) + ((FIRST + q + AHEAD) // 2 + 1))
                    drain_odd(c, q % 2, (rd * (SLOTS // 2) + (FIRST + q) // 2) * (16 * NT))
            for c in range(CH - AHEAD, CH):
                drain_odd(c, c % 2, (c // 2) * (16 * NT))

        @block.tensor
        def _(pe):
            def mm(o, l, r, start=True):
                return pe.matmul(o, l, r, start=start, stop=True, skip_group_check=True)

            def turn(bank, src):
                for j in range(J):
                    last = pe.transpose(bank[:, P * j:P * j + P], src[:, P * j:P * j + P], ident[:, :])
                return last

            pe.wait_ge(s_prep, n_prep[0])
            pe.wait_ge(s_const, n_const[0])

            def front_seqT(i):
                for u in range(U):
                    n = i * U + u
                    if not isinstance(i, int) or i > 0:
                        pe.wait_ge(s_PT, (i - 1) * U + u + 1)
                    pe.wait_ge(s_seq, n + 1)
                    turn(front[u], seq[:, u, :]).then_inc(p_seqT, 1)

            def front_keys(i):
                for u in range(U):
                    pe.wait_ge(s_seqT, i * U + u + 1)
                    mm(front[u][:, :], wbd[:, WK0, :], seqT[:, u, :]).then_inc(p_K, 1)

            def front_values(i):
                for u in range(U):
                    pe.wait_ge(s_K, i * U + u + 1)
                    mm(front[u][:, :], ones3[:, :], bv_rows[0:3, :])
                    for j in range(J):
                        last = mm(front[u][:, P * j:P * j + P], seqT[:, u, P * j:P * j + P], wbd[:, WV0, :], False)
                    last.then_inc(p_V, 1)

            def front_koffT(i):
                pe.wait_ge(s_V, i * U + 1)
                pe.wait_ge(s_koff, i + 1)
                pe.transpose(front[0][0:U * T, 0:P], koff[:, :], ident[:, :]).then_inc(p_koff, 1)

            def front_xT(i, groups):
                pe.wait_ge(s_koffT, i + 1)
                for u in groups:
                    n = i * U + u
                    pe.wait_ge(s_V, n + 1)
                    pe.wait_ge(s_xn, n + 1)
                    turn(front[u], xn[:, u, :]).then_inc(p_xT, 1)

            def front_query(i):
                for u in range(U):
                    pe.wait_ge(s_xT, i * U + u + 1)
                    mm(front[u][:, :], wbd[:, WQ0, :], xT[:, u, :]).then_inc(p_Q, 1)

            def front_scores(i, u):
                pe.wait_ge(s_Q, i * U + u + 1)
                for j in range(J):
                    mm(front[u][:, P * j:P * j + P], sel1[:, (u * J + j) * P:(u * J + j) * P + P],
                       koffT[:, :], j == 0)
                for h in range(2):
                    a, b = D * h, D * h + D
                    for c in range(T):
                        last = mm(front[u][a:b, D * c:D * c + D], QT[a:b, u, D * c:D * c + D],
                                  KT[a:b, u, D * c:D * c + D], False)
                last.then_inc(p_S, 1)

            def front_turn(i, groups):
                for u in groups:
                    pe.wait_ge(s_P, i * U + u + 1)
                    turn(front[u], att[:, u, :]).then_inc(p_PT, 1)

            def back_room(i, u, before, same):
                if u < U - 1:
                    pe.wait_ge(before, i * U + u + 2)
                else:
                    pe.wait_ge(same, i * U + 1)

            def back_hidden(i):
                for u in range(U):
                    back_room(i, u, s_x2T, s_H)
                    pe.wait_ge(s_x2T, i * U + u + 1)
                    mm(back(2, u)[:, :], wbd[:, W10, :], x2T[:, u, :]).then_inc(p_H, 1)

            def back_out(i, u):
                back_room(i, u, s_H, s_seq2T)
                pe.wait_ge(s_H, i * U + u + 1)
                mm(back(3, u)[:, :], wbd[:, W20, :], HT[:, u, :]).then_inc(p_Y, 1)

            def last_weighted(i):
                pe.wait_ge(c_QB, i + 1)
                mm(spare[:, 0:P], wbd[:, WKT1, :], QB[:, :, :].rearrange("p u c -> p (u c)")).then_inc(c_pa, 1)

            def last_scores(i):
                pe.wait_ge(c_kT, i + 1)
                for j in range(J):
                    mm(spare[:, P * j:P * j + P], sel2[:, P * j:P * j + P], koffT2[:, :], j == 0)
                mm(spare[:, :], QB[:, :, :].rearrange("p u c -> p (u c)"), bkrep[:, :], False)
                for u in range(U):
                    last = mm(spare[ROWS * u:ROWS * u + ROWS, :], AB[:, u, :], seq2T[:, u, :], False)
                last.then_inc(c_pS, 1)

            def last_turn(i):
                pe.wait_ge(c_P, i + 1)
                turn(spare, s2[:, :]).then_inc(c_pPT, 1)

            def last_attend(i):
                pe.wait_ge(c_PT, i + 1)
                for u in range(U):
                    for j in range(J):
                        last = mm(spare[ROWS * u:ROWS * u + ROWS, 0:P],
                                  PT2[:, P * j + ROWS * u:P * j + ROWS * u + ROWS],
                                  seq2[:, u, P * j:P * j + P], j == 0)
                last.then_inc(c_pO, 1)

            def last_back(i):
                pe.wait_ge(c_O, i + 1)
                pe.transpose(spare[:, 0:P], o2[:, :], ident[:, :]).then_inc(c_pOT, 1)

            def back_z(i):
                for u in range(U):
                    if not isinstance(i, int) or i > 0:
                        if u < U - 1:
                            pe.wait_ge(s_seq2, i * U)
                        else:
                            pe.wait_ge(c_var, i)
                    pe.wait_ge(s_PT, i * U + u + 1)
                    for j in range(J):
                        mm(back(0, u)[:, P * j:P * j + P], xT[:, u, P * j:P * j + P], center[:, :], j == 0)
                    for s in range(2):
                        a, b = D * s, D * s + D
                        for t in range(T):
                            last = mm(back(0, u)[a:b, D * t:D * t + D], PT[a:b, u, D * t:D * t + D],
                                      V[a:b, u, D * t:D * t + D], False)
                    last.then_inc(p_z, 1)

            def back_x2T(i, groups):
                for u in groups:
                    if u == U - 1:
                        pe.wait_ge(s_x2T, i * U + 1)
                    pe.wait_ge(s_zn, i * U + u + 1)
                    turn(back(1, u), zq[:, u, :]).then_inc(p_x2T, 1)

            def back_tokens(i, groups):
                for u in groups:
                    back_room(i, u, s_seq2T, s_seq2)
                    pe.wait_ge(s_seq2T, i * U + u + 1)
                    turn(back(4, u), seq2T[:, u, :]).then_inc(p_seq2, 1)

            def last_centre(i):
                if not isinstance(i, int) or i > 0:
                    pe.wait_ge(c_OT, i)
                pe.wait_ge(c_last, i + 1)
                mm(spare[:, 0:LC], center[:, :], xl[:, 0, :]).then_inc(c_pc, 1)

            def last_var(i):
                pe.wait_ge(c_sq, i + 1)
                mm(spare[:, 0:LC], mean_m[:, :], xl[:, 2, :]).then_inc(c_pv, 1)

            def last_query(i, b):
                if b:
                    pe.wait_ge(s_zn, (i + 2) * U)
                pe.wait_ge(c_x, i + 1)
                mm(spare[:, 0:LC], wbd[:, WQ1, :], xl[:, 7, :]).then_inc(c_pq, 1)

            def last_keys(i):
                pe.wait_ge(c_AB, i + 1)
                pe.wait_ge(s_koff2, i + 1)
                pe.transpose(spare[0:U * T, 0:P], koff2[:, :], ident[:, :]).then_inc(c_pk, 1)

            def body(i, a, b, c):
                if a:
                    front_seqT(i)
                if c:
                    last_var(i - 2)
                if b:
                    back_z(i - 1)
                if a:
                    front_keys(i)
                    front_values(i)
                    front_koffT(i)
                if b:
                    back_x2T(i - 1, (0, 1, 2))
                if a:
                    front_xT(i, (0, 1))
                if b:
                    back_x2T(i - 1, (3,))
                if c:
                    last_query(i - 2, b)
                if a:
                    front_xT(i, (2, 3))
                if c:
                    last_weighted(i - 2)
                if b:
                    back_hidden(i - 1)
                if c:
                    last_keys(i - 2)
                if a:
                    front_query(i)
                if c:
                    last_scores(i - 2)
                for u in range(U):
                    if a:
                        front_scores(i, u)
                    if b:
                        back_out(i - 1, u)
                if c:
                    last_turn(i - 2)
                if a:
                    front_turn(i, (0,))
                if c:
                    last_attend(i - 2)
                if a:
                    front_turn(i, (1,))
                if c:
                    last_back(i - 2)
                if b:
                    back_tokens(i - 1, (0, 1, 2))
                if a:
                    front_turn(i, (2,))
                if b:
                    back_tokens(i - 1, (3,))
                    last_centre(i - 1)
                if a:
                    front_turn(i, (3,))

            body(0, True, False, False)
            body(1, True, True, False)
            with pe.Fori(2, STEPS) as i:
                body(i, True, True, True)
            body(STEPS, False, True, True)
            body(STEPS + 1, False, False, True)

            pe.wait_ge(c_XL, STEPS)
            pe.wait_ge(s_seq2, STEPS * U)
            mm(hi[1][:, 0:QL], mean_m[:, :], XL[:, :]).then_inc(e_pe, 1)
            pe.wait_ge(c_OT, STEPS)
            mm(hi[0][:, 0:QL], wbd[:, WV1, :], OT[:, :]).then_inc(e_pe, 1)
            pe.wait_ge(e_dve, E_SUM)
            mm(lo[0][:, 0:QL], center[:, :], za).then_inc(e_pe, 1)
            pe.wait_ge(e_act, 1)
            mm(lo[1][:, 0:QL], mean_m[:, :], zs).then_inc(e_pe, 1)
            pe.wait_ge(e_act, 3)
            mm(lo[2][:, 0:QL], wbd[:, W11, :], zx).then_inc(e_pe, 1)
            pe.wait_ge(e_act, 4)
            mm(lo[3][:, 0:QL], wbd[:, W21, :], zh).then_inc(e_pe, 1)
            pe.wait_ge(e_dve, E_OUT)
            mm(hi[2][:, 0:QL], center[:, :], zy).then_inc(e_pe, 1)
            pe.wait_ge(e_act, 5)
            mm(hi[3][:, 0:QL], mean_m[:, :], zs).then_inc(e_pe, 1)

            pe.wait_ge(f_split, 1)

            def product(c, slot):
                pe.wait_ge(i_xy, c + 1)
                pe.wait_ge(i_hs, c + 1)
                for t in range(NT):
                    for half in range(2):
                        b = banks[2 * t + half]
                        if not isinstance(c, int) or c > 0:
                            pe.wait_ge(o_even if half == 0 else o_odd, (c - 1) * NT + t + 1)
                        xs = ix[slot][:, NB * half:NB * half + NB]
                        ys = iy[slot][:, NB * half:NB * half + NB]
                        mm(b[:, 0:NB], f_hi[:, P * t:P * t + P], xs)
                        mm(b[:, 0:NB], f_mid[:, P * t:P * t + P], xs, False)
                        last = mm(b[:, 0:NB], f_hl[:, P * t:P * t + P], ys, False)
                        last.then_inc(i_mm, 1)

            product(0, 0)
            with pe.Fori(0, CH // SLOTS) as rd:
                for q in range(SLOTS):
                    product(rd * SLOTS + (1 + q), (1 + q) % SLOTS)


def kernel(r_input_ids, L0_rec_item_emb, L0_rec_pos_emb, L0_rec_ln1_g, L0_rec_ln1_b, L0_rec_Wq, L0_rec_bq,
           L0_rec_Wk, L0_rec_bk, L0_rec_Wv, L0_rec_bv, L0_rec_ln2_g, L0_rec_ln2_b, L0_rec_W1, L0_rec_b1,
           L0_rec_W2, L0_rec_b2, L0_rec_lnf_g, L0_rec_lnf_b, L0_rec_out_item_emb):
    import numpy as np
    import concourse.bacc as bacc
    from concourse.bass_utils import run_bass_kernel_spmd

    a = lambda x: np.ascontiguousarray(x)
    ids = np.asarray(r_input_ids)
    nb = ids.shape[0]
    groups = nb // (2 * T)
    g1, b1_, bq, bk, bv = (np.asarray(x) for x in (L0_rec_ln1_g, L0_rec_ln1_b, L0_rec_bq, L0_rec_bk, L0_rec_bv))
    g2, b2_, f1, f2 = (np.asarray(x) for x in (L0_rec_ln2_g, L0_rec_ln2_b, L0_rec_b1, L0_rec_b2))
    wq, wk, wv, w1, w2 = (np.asarray(x) for x in (L0_rec_Wq, L0_rec_Wk, L0_rec_Wv, L0_rec_W1, L0_rec_W2))
    vec_list = [g1[0], b1_[0], bq[0], bk[0], g2[0], b2_[0], f1[0], f2[0],
                g1[1], b1_[1], bq[1], bv[1], g2[1], b2_[1], f1[1], f2[1],
                np.asarray(L0_rec_lnf_g), np.asarray(L0_rec_lnf_b), bk[1]]
    w_list = [wq[0], wk[0], wv[0], w1[0], w2[0], wq[1], wk[1].T, wv[1], w1[1], w2[1]]

    f = np.float32
    eye = np.eye(P, dtype=f)
    blocks = np.kron(np.eye(2, dtype=f), np.ones((D, D), f))
    q = np.arange(P) % D
    causal = np.where(np.arange(D)[None, :] <= q[:, None], f(3e38), f(NEG)).astype(f)
    sel1 = np.zeros((U, T, U, J, 2, D), f)
    sel2 = np.zeros((U, T, J, U, ROWS), f)
    diag2 = np.full((U, ROWS, J, 2, D), f(3e38), f)
    for u in range(U):
        for j in range(J):
            for h in range(2):
                sel1[u, 2 * j + h, u, j, h, :] = 1
                for jj in range(J):
                    for s in range(2):
                        m = (h * J + jj) * 2 + s
                        sel2[u, 2 * j + h, j, u, m] = 1
                        if (jj, s) != (j, 0):
                            diag2[u, m, j, 0, :] = -1e38
                        if (jj, s) != (j, 1):
                            diag2[u, m, j, 1, :] = -1e38
    arrays = {
        "ids_tok": a(ids.reshape(-1, P).T),
        "ids_last": a(ids[:, -1].reshape(groups, J, 2, 2).transpose(2, 0, 1, 3).reshape(2, -1)),
        "item_emb": a(L0_rec_item_emb),
        "vecs": a(np.stack(vec_list, 1)),
        "weights": a(np.stack(w_list, 1)),
        "pos": a(L0_rec_pos_emb),
        "bv_row": a(bv[0:1]),
        "ln_rows": a(np.stack([g1[0], b1_[0]])),
        "items_t": a(np.asarray(L0_rec_out_item_emb).T),
        "ident_c": eye,
        "center_c": (eye - blocks / D).astype(f),
        "mean_c": (blocks / D).astype(f),
        "causal_c": causal,
        "diag2_c": diag2.reshape(P, W),
        "sel1_c": sel1.reshape(U * T, -1),
        "sel2_c": sel2.reshape(U * T, -1),
    }
    nc = bacc.Bacc("TRN2", target_bir_lowering=False, num_devices=1)
    args = [nc.dram_tensor(k, v.shape, mybir.dt.from_np(v.dtype), kind="ExternalInput").ap()
            for k, v in arrays.items()]
    out = nc.dram_tensor("scores_out", (nb, L0_rec_out_item_emb.shape[0]), F32, kind="ExternalOutput").ap()
    build(nc, *args, out)
    r = run_bass_kernel_spmd(nc, [arrays], core_ids=[0])
    return r.results[0]["scores_out"]
```
